# Optimizing a Trainium2 kernel written in Bass

```python
import numpy as np
import jax
import jax.numpy as jnp

def _softmax(x, axis=-1):
    return jax.nn.softmax(x, axis=axis)

def _gelu(x):
    return jax.nn.gelu(x, approximate=True)

def _silu(x):
    return jax.nn.silu(x)

def _sigmoid(x):
    return jax.nn.sigmoid(x)

def _layernorm(x, axis=-1, eps=1e-05):
    m = jnp.mean(x, axis=axis, keepdims=True)
    v = jnp.var(x, axis=axis, keepdims=True)
    return (x - m) / jnp.sqrt(v + eps)

def _scatter_add(tgt, idx, src, axis=0):
    return tgt.at[idx].add(src)

def _segment_sum(src, seg, n):
    return jax.ops.segment_sum(src, seg, n)
kernel_name = 'mk_macaron_d1_jaxref_r8_a5b7fc'

def setup_inputs(seed: int=0):
    np.random.seed(seed)
    _w = jnp.asarray

    def _L0_attn_setup():
        import jax, jax.numpy as jnp
        import numpy as np
        from jax import lax
        B, N, D = (4, 512, 256)
        E = 128
        H = D // E
        CHUNK = 64
        EPS = 1e-06

        def rmsnorm(x, w):
            var = jnp.mean(jnp.square(x), axis=-1, keepdims=True)
            return x * lax.rsqrt(var + EPS) * w

        def chunked_gla(q, v, log_f):
            b, n, h, e = q.shape
            nc = n // CHUNK
            k = 1.0 - jnp.exp(log_f)

            def to_chunks(t):
                return t.reshape(b, nc, CHUNK, h, e).transpose(1, 0, 2, 3, 4)
            qs, ks_, vs, lfs = map(to_chunks, (q, k, v, log_f))
            A = jnp.cumsum(lfs, axis=2)
            mask = jnp.tril(jnp.ones((CHUNK, CHUNK), dtype=bool))

            def step(S, xs):
                qc, kc, vc, Ac = xs
                q_dec = qc * jnp.exp(Ac)
                k_dec = kc * jnp.exp(-Ac)
                scores = jnp.einsum('bthe,bshe->bhts', q_dec, k_dec)
                scores = jnp.where(mask[None, None], scores, 0.0)
                o_intra = jnp.einsum('bhts,bshe->bthe', scores, vc)
                o_inter = jnp.einsum('bthe,bhef->bthf', q_dec, S)
                A_last = Ac[:, -1]
                k_rem = kc * jnp.exp(A_last[:, None] - Ac)
                S_new = jnp.exp(A_last)[..., None] * S + jnp.einsum('bthe,bthf->bhef', k_rem, vc)
                return (S_new, o_intra + o_inter)
            S0 = jnp.zeros((b, h, e, e), dtype=q.dtype)
            _, o = lax.scan(step, S0, (qs, ks_, vs, A))
            return o.transpose(1, 0, 2, 3, 4).reshape(b, n, h, e)
        key = jax.random.key(seed)
        ks = jax.random.split(key, 6)
        std = 0.02
        x = jax.random.normal(ks[0], (B, N, D), dtype=jnp.float32)
        Wq = jax.random.normal(ks[1], (D, D), dtype=jnp.float32) * std
        Wk = jax.random.normal(ks[2], (D, D), dtype=jnp.float32) * std
        Wv = jax.random.normal(ks[3], (D, D), dtype=jnp.float32) * std
        Wo = jax.random.normal(ks[4], (D, D), dtype=jnp.float32) * std
        norm_w = jnp.ones((D,), dtype=jnp.float32)
        return {'x': x, 'Wq': Wq, 'Wk': Wk, 'Wv': Wv, 'Wo': Wo, 'norm_w': norm_w}
    _L0_attn_in = _L0_attn_setup()

    def _L0_ffn_setup():
        import jax, jax.numpy as jnp
        import numpy as np
        TOP_K = 4

        def _silu_and_mul(gu):
            g, u = jnp.split(gu, 2, axis=-1)
            return jax.nn.silu(g) * u
        key = jax.random.key(seed)
        ks = jax.random.split(key, 7)
        H, E, I, Is = (256, 16, 176, 704)
        s = 0.02
        return {'hidden_states': jax.random.normal(ks[0], (4, 128, H), dtype=jnp.float32), 'gate_w': jax.random.normal(ks[1], (E, H), dtype=jnp.float32) * s, 'sgate_w': jax.random.normal(ks[2], (1, H), dtype=jnp.float32) * s, 'w13': jax.random.normal(ks[3], (E, 2 * I, H), dtype=jnp.float32) * s, 'w2': jax.random.normal(ks[4], (E, H, I), dtype=jnp.float32) * s, 'shared_gate_up_w': jax.random.normal(ks[5], (2 * Is, H), dtype=jnp.float32) * s, 'shared_down_w': jax.random.normal(ks[6], (H, Is), dtype=jnp.float32) * s}
    _L0_ffn_in = _L0_ffn_setup()
    _d = {'L0_attn_x': _L0_attn_in['x'], 'L0_attn_Wq': _L0_attn_in['Wq'], 'L0_attn_Wk': _L0_attn_in['Wk'], 'L0_attn_Wv': _L0_attn_in['Wv'], 'L0_attn_Wo': _L0_attn_in['Wo'], 'L0_attn_norm_w': _L0_attn_in['norm_w'], 'L0_ffn_gate_w': _L0_ffn_in['gate_w'], 'L0_ffn_sgate_w': _L0_ffn_in['sgate_w'], 'L0_ffn_w13': _L0_ffn_in['w13'], 'L0_ffn_w2': _L0_ffn_in['w2'], 'L0_ffn_shared_gate_up_w': _L0_ffn_in['shared_gate_up_w'], 'L0_ffn_shared_down_w': _L0_ffn_in['shared_down_w']}
    _x0 = _d['L0_attn_x']
    _d['L0_attn_x'] = jax.random.normal(jax.random.fold_in(jax.random.key(seed), 1), (1, 1024, 256), dtype=_x0.dtype)
    del _x0
    return _d

def reference(L0_attn_x, L0_attn_Wq, L0_attn_Wk, L0_attn_Wv, L0_attn_Wo, L0_attn_norm_w, L0_ffn_gate_w, L0_ffn_sgate_w, L0_ffn_w13, L0_ffn_w2, L0_ffn_shared_gate_up_w, L0_ffn_shared_down_w):

    def _L0_attn_ref(x, Wq, Wk, Wv, Wo, norm_w):
        import jax, jax.numpy as jnp
        import numpy as np
        from jax import lax
        B, N, D = (4, 512, 256)
        E = 128
        H = D // E
        CHUNK = 64
        EPS = 1e-06

        def rmsnorm(x, w):
            var = jnp.mean(jnp.square(x), axis=-1, keepdims=True)
            return x * lax.rsqrt(var + EPS) * w

        def chunked_gla(q, v, log_f):
            b, n, h, e = q.shape
            nc = n // CHUNK
            k = 1.0 - jnp.exp(log_f)

            def to_chunks(t):
                return t.reshape(b, nc, CHUNK, h, e).transpose(1, 0, 2, 3, 4)
            qs, ks_, vs, lfs = map(to_chunks, (q, k, v, log_f))
            A = jnp.cumsum(lfs, axis=2)
            mask = jnp.tril(jnp.ones((CHUNK, CHUNK), dtype=bool))

            def step(S, xs):
                qc, kc, vc, Ac = xs
                q_dec = qc * jnp.exp(Ac)
                k_dec = kc * jnp.exp(-Ac)
                scores = jnp.einsum('bthe,bshe->bhts', q_dec, k_dec)
                scores = jnp.where(mask[None, None], scores, 0.0)
                o_intra = jnp.einsum('bhts,bshe->bthe', scores, vc)
                o_inter = jnp.einsum('bthe,bhef->bthf', q_dec, S)
                A_last = Ac[:, -1]
                k_rem = kc * jnp.exp(A_last[:, None] - Ac)
                S_new = jnp.exp(A_last)[..., None] * S + jnp.einsum('bthe,bthf->bhef', k_rem, vc)
                return (S_new, o_intra + o_inter)
            S0 = jnp.zeros((b, h, e, e), dtype=q.dtype)
            _, o = lax.scan(step, S0, (qs, ks_, vs, A))
            return o.transpose(1, 0, 2, 3, 4).reshape(b, n, h, e)
        b, n, d = x.shape
        q = jax.nn.silu(x @ Wq.T)
        f = jax.nn.sigmoid(x @ Wk.T)
        log_f = jax.nn.log_sigmoid(f)
        v = x @ Wv.T
        q, v, log_f = (t.reshape(b, n, H, E) for t in (q, v, log_f))
        o = chunked_gla(q, v, log_f)
        o = o.reshape(b, n, d)
        o = rmsnorm(o, norm_w)
        return o @ Wo.T

    def _L0_ffn_ref(hidden_states, gate_w, sgate_w, w13, w2, shared_gate_up_w, shared_down_w):
        import jax, jax.numpy as jnp
        import numpy as np
        TOP_K = 4

        def _silu_and_mul(gu):
            g, u = jnp.split(gu, 2, axis=-1)
            return jax.nn.silu(g) * u
        B, S, H = hidden_states.shape
        x = hidden_states.reshape(-1, H)
        E = gate_w.shape[0]
        shared = _silu_and_mul(x @ shared_gate_up_w.T) @ shared_down_w.T
        shared = shared * jax.nn.sigmoid(x @ sgate_w.T)
        router_logits = x @ gate_w.T
        routing_weights = jax.nn.softmax(router_logits.astype(jnp.float32), axis=-1)
        topk_w, topk_ids = jax.lax.top_k(routing_weights, TOP_K)

        def body(acc, ew):
            w13_e, w2_e, e = ew
            coef = jnp.sum(jnp.where(topk_ids == e, topk_w, 0.0), axis=-1)
            h = _silu_and_mul(x @ w13_e.T)
            acc = acc + (h @ w2_e.T).astype(jnp.float32) * coef[:, None]
            return (acc, None)
        init = jnp.zeros((x.shape[0], H), dtype=jnp.float32)
        sparse_out, _ = jax.lax.scan(body, init, (w13, w2, jnp.arange(E)))
        out = shared + sparse_out.astype(x.dtype)
        return out.reshape(B, S, H)
    x = L0_attn_x
    x = x + 0.5 * _L0_ffn_ref(_layernorm(x, axis=-1), L0_ffn_gate_w, L0_ffn_sgate_w, L0_ffn_w13, L0_ffn_w2, L0_ffn_shared_gate_up_w, L0_ffn_shared_down_w)
    x = x + _L0_attn_ref(_layernorm(x, axis=-1), L0_attn_Wq, L0_attn_Wk, L0_attn_Wv, L0_attn_Wo, L0_attn_norm_w)
    x = x + 0.5 * _L0_ffn_ref(_layernorm(x, axis=-1), L0_ffn_gate_w, L0_ffn_sgate_w, L0_ffn_w13, L0_ffn_w2, L0_ffn_shared_gate_up_w, L0_ffn_shared_down_w)
    return x

_drawn_inputs = setup_inputs


def setup_inputs(seed=0):
    import zlib

    import numpy as np

    out = dict(_drawn_inputs(seed))
    spreads = {'L0_attn_norm_w': (1.0, 0.2)}
    factors = {'L0_attn_Wk': 5.016,
     'L0_ffn_gate_w': 8.0,
     'L0_ffn_sgate_w': 8.0,
     'L0_ffn_w13': 8.0,
     'L0_ffn_w2': 8.0,
     'L0_ffn_shared_gate_up_w': 4.254,
     'L0_ffn_shared_down_w': 4.256}
    for name, (base, spread) in spreads.items():
        noise = np.random.default_rng([zlib.crc32(name.encode()), seed]).standard_normal(out[name].shape)
        drawn = base * np.exp(spread * noise) if base else spread * noise
        out[name] = jnp.asarray(drawn.astype(out[name].dtype))
    for name, factor in factors.items():
        out[name] = (out[name] * factor).astype(out[name].dtype)
    return out
```

```python
from contextlib import ExitStack

import numpy as np

import concourse.bass as bass
from concourse import mybir

F32 = mybir.dt.float32
F32R = mybir.dt.float32r
I32 = mybir.dt.int32
ALU = mybir.AluOpType
ACT = mybir.ActivationFunctionType
AX = mybir.AxisListType

P = 128
N = 1024
D = 256
KD = D // P
HALF = 512
NE, TOPK = 16, 4
FE, FS = 176, 704
GRP = 16
NJ = -(-(NE * FE + FS) // P)
NG = NJ * P // GRP
WC = 2 * KD * P + D
NC = NE + 1
NT = N // P
CH = 64
NH = 2
LN_EPS, RMS_EPS = 1e-5, 1e-6
UNITS = 2 * NJ
NM = NJ // 2

C_ONES, C_ID, C_TRI, C_REM, C_CHUNK = 0, 128, 256, 512, 640
C_ALL = 642


def spread(a, axis, n):
    a = a.unsqueeze(axis)
    shape = list(a.shape)
    shape[axis] = n
    return a.broadcast_to(shape)


def macaron(nc, xT, wffn, wgate, wkqv, woT, normw, consts, out):
    ctx = ExitStack()

    def sb(name, shape, dt=F32):
        return ctx.enter_context(nc.sbuf_tensor(name, shape, dt))

    def sem(name):
        return ctx.enter_context(nc.semaphore(name))

    with ctx:
        ps = ctx.enter_context(nc.psum_tensor("ps", [P, 8, HALF], F32))
        coef_dram = nc.dram_tensor("coef_groups", [NG, N], F32, kind="Internal").ap()
        cst = sb("cst", [P, C_ALL])
        X = sb("X", [P, KD, N])
        XN = sb("XN", [P, KD, N])
        XH = sb("XH", [P, KD, N], F32R)
        XL = sb("XL", [P, KD, N], F32R)
        WR = sb("WR", [P, NJ, WC])
        WH = [sb(f"WH{p}", [P, WC], F32R) for p in range(2)]
        WL = [sb(f"WL{p}", [P, WC], F32R) for p in range(2)]
        WG = sb("WG", [P, KD, NC])
        WA = sb("WA", [P, KD, 3 * D])
        WO = sb("WO", [P, NH, D])
        nw = sb("nw", [P, NH])
        eps_ln = sb("eps_ln", [P, 1])
        eps_rms = sb("eps_rms", [P, 1])
        one = sb("one", [P, 1])
        ar = sb("ar", [P, 15 * HALF])

        def area(at, n):
            return ar[:, at:at + n]

        Dv = [sb(f"Dv{h}", [P, KD, HALF]) for h in range(2)]
        Sq = [area(h * 2 * HALF, 2 * HALF).rearrange("p (k n) -> p k n", k=KD) for h in range(2)]
        Lv = [area((4 + h) * HALF, HALF) for h in range(2)]
        Rs = [area((6 + h) * HALF, HALF) for h in range(2)]
        CB = [area(2 * p * HALF, N) for p in range(2)]
        Sg = [area((4 + h) * HALF, HALF) for h in range(2)]
        Tc = [area((6 + h) * HALF, HALF) for h in range(2)]
        Hf = [area((8 + h) * HALF, HALF) for h in range(2)]
        HH = [sb(f"HH{h}", [P, HALF], F32R) for h in range(2)]
        HL = [sb(f"HL{h}", [P, HALF], F32R) for h in range(2)]
        lg = sb("lg", [P, NT, NE])
        pe_ = sb("pe_", [P, NT, NE])
        pr = sb("pr", [P, NT, NE])
        m8 = sb("m8", [P, NT, 8])
        t1 = sb("t1", [P, NT])
        t2 = sb("t2", [P, NT])
        sgt = sb("sgt", [P, NT])
        gt = sb("gt", [P, NT, NE])
        eq = sb("eq", [P, NT, NE])
        cs = [sb(f"cs{i}", [P, NT, 2 * NE]) for i in range(2)]
        cf = sb("cf", [P, NT, NC])
        cT = sb("cT", [NC, N])
        XT = [sb(f"XT{p}", [P, KD, P]) for p in range(2)]
        Ea = area(0, 512)
        Aa = area(512, 512)
        Ra = [area(1024 + 512 * p, 512) for p in range(2)]
        Qa = [area(2048 + 256 * p, 256) for p in range(2)]
        Ga = area(2560, 256)
        La = [area(2816 + 256 * p, 256) for p in range(2)]
        Xa = [area(3328 + 256 * p, 256) for p in range(2)]
        E13 = [area(3840 + 512 * p, 512) for p in range(2)]
        E2 = [area(4864 + 256 * p, 256) for p in range(2)]
        Ka = [area(5376 + 256 * p, 256) for p in range(2)]
        QD = [area(5888 + 256 * p, 256) for p in range(2)]
        KD_ = [area(6400 + 256 * p, 256) for p in range(2)]
        KR = [area(6912 + 256 * p, 256) for p in range(2)]
        QKT = [Dv[0][:, p, :].rearrange("p (i n) -> p i n", i=4) for p in range(2)]
        Va = [Dv[1][:, 0, p * D:(p + 1) * D] for p in range(2)]
        DC = [sb(f"DC{p}", [P, NH, 2]) for p in range(2)]
        SM = [sb(f"SM{p}", [P, NH * P]) for p in range(2)]
        ST = [sb(f"ST{i}", [P, NH, P]) for i in range(4)]
        OT = XN

        ones = cst[:, C_ONES:C_ONES + P]
        ident = cst[:, C_ID:C_ID + P]
        tri = cst[:, C_TRI:C_TRI + P]
        tri2 = cst[:, C_TRI:C_TRI + NH * P].bitcast(I32)
        rem = cst[:, C_REM:C_REM + P]
        chunk = cst[:, C_CHUNK:C_CHUNK + 2]

        s_xin = [sem(f"s_xin{h}") for h in range(2)]
        s_cst, s_wg, s_wa, s_out, s_cg = (sem(n) for n in ("s_cst", "s_wg", "s_wa", "s_out", "s_cg"))
        s_wr = [sem(f"s_wr{p}") for p in range(2)]
        s_cb = [sem(f"s_cb{p}") for p in range(2)]
        s_set = sem("s_set")
        s_mean, s_d, s_sq, s_var, s_ln, s_rs, s_xn, s_xh, s_xl, s_xr = (
            sem(n) for n in "s_mean s_d s_sq s_var s_ln s_rs s_xn s_xh s_xl s_xr".split())
        s_lg, s_lgc, s_ex, s_sgx, s_coef, s_ct, s_cts, s_chain = (
            sem(n) for n in "s_lg s_lgc s_ex s_sgx s_coef s_ct s_cts s_chain".split())
        s_wh, s_wl, s_g, s_u, s_si, s_tc, s_h, s_hh, s_hl, s_l2 = (
            sem(n) for n in "s_wh s_wl s_g s_u s_si s_tc s_h s_hh s_hl s_l2".split())
        (a_xt, a_kq, a_z, a_e, a_v, a_a, a_r, a_q, a_g, a_L, a_ex, a_b, a_e3, a_k, a_qk, a_kr, a_c, a_qkT,
         a_kv, a_sm, a_s1, a_st, a_o, a_ow, a_wo) = (
            sem("a_" + n) for n in ("xt kq z e v a r q g L ex b e3 k qk kr c qkT kv sm s1 st o ow wo").split())
        f_sq, f_ss, f_ln, f_r, f_y, f_t = (sem("f_" + n) for n in "sq ss ln r y t".split())

        block = ctx.enter_context(nc.Block())

        def wait(eng, s, v):
            if isinstance(v, int) and v <= 0:
                return
            eng.wait_ge(s, v)

        def half(h):
            return slice(h * HALF, (h + 1) * HALF)

        def kv_bank(h, c):
            return ps[:, 2, (NH + h) * P:(NH + h + 1) * P] if c == 0 else ps[:, 7, h * P:(h + 1) * P]

        def turns(eng, body, last):
            body(0)
            with eng.Fori(1, last) as m:
                body(m)
            body(last)

        @block.sync
        def _(sp):
            def load_w(j, p):
                sp.dma_start(WR[:, bass.ds(j, 1), :], wffn[bass.ds(j, 1), :, :].rearrange("a p n -> p a n")).then_inc(s_wr[p], 16)

            def load_cb(j, p):
                src = coef_dram[bass.ds(j * (P // GRP), P // GRP), :]
                sp.dma_start(CB[p], spread(src, 1, GRP)).then_inc(s_cb[p], 16)

            for h in range(2):
                sp.dma_start(X[:, :, half(h)], xT[:, :, half(h)]).then_inc(s_xin[h], 16)
                if h == 0:
                    sp.dma_start(cst[:, :], consts).then_inc(s_cst, 16)
            sp.dma_start(WG[:, :, :], wgate).then_inc(s_wg, 16)
            load_w(0, 0)
            load_w(1, 1)
            sp.dma_start(WA[:, :, :], wkqv).then_inc(s_wa, 16)
            sp.dma_start(WO[:, :, :], woT).then_inc(s_wa, 16)
            sp.dma_start(nw[:, :], normw).then_inc(s_wa, 16)
            for p in range(2):
                sp.wait_ge(s_wr[p], 16)
                load_w(2 + p, p)

            for f in range(2):
                sp.wait_ge(s_cts, f + 1)
                er = NE * (FE // GRP)
                rows = coef_dram[0:er, :].rearrange("(e r) n -> e r n", r=FE // GRP)
                sp.dma_start(rows, spread(cT[0:NE, :], 1, FE // GRP)).then_inc(s_cg, 16)
                sp.dma_start(coef_dram[er:NG, :].rearrange("(a r) n -> a r n", a=1),
                             spread(cT[NE:NC, :], 1, NG - er)).then_inc(s_cg, 16)
                sp.wait_ge(s_cg, 32 * (f + 1))
                for p in range(2):
                    load_cb(p, p)

                def turn(m, weights):
                    for p in range(2):
                        if weights:
                            sp.wait_ge(s_wr[p], 16 * (m + 2))
                            load_w(2 * m + 4 + p, p)
                        sp.wait_ge(s_tc, UNITS * f + 4 * m + 2 + 2 * p)
                        load_cb(2 * m + 2 + p, p)

                if f == 0:
                    with sp.Fori(0, NM - 2) as m:
                        turn(m, True)
                    turn(NM - 2, False)
                else:
                    with sp.Fori(0, NM - 1) as m:
                        turn(m, False)

            for h in range(2):
                sp.wait_ge(s_xr, 5 + h)
                sp.dma_start(out[:, :, half(h)], X[:, :, half(h)]).then_inc(s_out, 16)
            sp.wait_ge(s_out, 32)

        @block.tensor
        def _(pe):
            def norm_stats(c):
                for h in range(2):
                    if c == 0:
                        if h == 0:
                            pe.wait_ge(s_cst, 16)
                        pe.wait_ge(s_xin[h], 16)
                    else:
                        pe.wait_ge(s_xr, 2 * (c - 1) + h + 1)
                    for k in range(KD):
                        mm = pe.matmul(ps[:, 4 + h, :], ones, X[:, k, half(h)], start=k == 0, stop=k == KD - 1)
                    mm.then_inc(s_mean, 1)
                for h in range(2):
                    pe.wait_ge(s_sq, 2 * c + h + 1)
                    for k in range(KD):
                        mm = pe.matmul(ps[:, 6 + h, :], ones, Sq[h][:, k, :], start=k == 0, stop=k == KD - 1)
                    mm.then_inc(s_var, 1)

            def logits(f):
                if f == 0:
                    pe.wait_ge(s_wg, 16)
                pe.wait_ge(s_xn, 4 * f + 2)
                for t in range(NT):
                    for k in range(KD):
                        mm = pe.matmul(ps[:, 0, t * NC:(t + 1) * NC], XN[:, k, t * P:(t + 1) * P], WG[:, k, :],
                                       start=k == 0, stop=k == KD - 1)
                mm.then_inc(s_lg, 1)

            def turn_coefs(f):
                pe.wait_ge(s_coef, f + 1)
                for t in range(NT):
                    mm = pe.transpose(ps[0:NC, 1 + t // 4, (t % 4) * P:(t % 4 + 1) * P], cf[:, t, :], ident)
                mm.then_inc(s_ct, 1)

            def first(f, u, j, p, h):
                if isinstance(u, int) and u < 2:
                    pe.wait_ge(s_xl, 2 * f + h + 1)
                if h == 0:
                    wait(pe, s_wl, NJ * f + j + 1)
                for what, bank, done, freed in ((0, 4, s_g, s_si), (1, 6, s_u, s_h)):
                    wait(pe, freed, UNITS * f + u - 1)
                    n = 0
                    for w, x in ((WH, XH), (WH, XL), (WL, XH)):
                        for k in range(KD):
                            col = (what * KD + k) * P
                            mm = pe.matmul(ps[:, bank + h, :], w[p][:, col:col + P], x[:, k, half(h)],
                                           start=n == 0, stop=n == 5)
                            n += 1
                    mm.then_inc(done, 1)

            def second(f, u, p, h, start, stop):
                wait(pe, s_hl, UNITS * f + u + 1)
                n = 0
                for w, x in ((WH, HH), (WH, HL), (WL, HH)):
                    for k in range(KD):
                        col = 2 * KD * P + k * P
                        mm = pe.matmul(ps[:, 2 * h + k, :], w[p][:, col:col + P], x[h][:, :],
                                       start=start and n < 2, stop=stop and n >= 4, skip_group_check=True)
                        n += 1
                mm.then_inc(s_l2, 1)

            def ffn(f):
                first(f, 0, 0, 0, 0)

                def turn(m):
                    for k in range(4):
                        k1 = k + 1
                        if not (isinstance(m, int) and m == NM - 1 and k == 3):
                            first(f, 4 * m + k1, 2 * m + k1 // 2, k1 // 2 % 2, k1 % 2)
                        if isinstance(m, int) and m == 0 and k == 0:
                            turn_coefs(f)
                        second(f, 4 * m + k, k // 2, k % 2, isinstance(m, int) and m == 0 and k < 2,
                               isinstance(m, int) and m == NM - 1 and k >= 2)
                turns(pe, turn, NM - 1)

            def attention():
                pe.wait_ge(s_wa, 48)

                def project(t, p):
                    wait(pe, a_xt, t + 1)
                    wait(pe, a_q, t)
                    for k in range(KD):
                        mm = pe.matmul(ps[:, 4, :], XT[p][:, k, :], WA[:, k, 0:2 * D], start=k == 0, stop=k == KD - 1)
                    mm.then_inc(a_kq, 1)
                    wait(pe, a_v, t)
                    for k in range(KD):
                        mm = pe.matmul(ps[:, 5, 0:D], XT[p][:, k, :], WA[:, k, 2 * D:3 * D], start=k == 0, stop=k == KD - 1)
                    mm.then_inc(a_z, 1)

                def sums(t, p):
                    wait(pe, a_L, t + 1)
                    wait(pe, a_e3, t)
                    pe.matmul(ps[:, 6, 0:D], tri, La[p], start=True, stop=True)
                    pe.matmul(ps[:, 6, D:2 * D], rem, La[p], start=True, stop=True)
                    for h in range(NH):
                        mm = pe.matmul(ps[:, 0, 2 * h:2 * h + 2], La[p][:, h * P:(h + 1) * P], chunk, start=True, stop=True)
                    mm.then_inc(a_b, 1)

                def turn_qk(t, p):
                    wait(pe, a_qk, t + 1)
                    wait(pe, a_qkT, t)
                    for i, src in enumerate((QD, KD_)):
                        for h in range(NH):
                            mm = pe.transpose(ps[:, 3, (2 * i + h) * P:(2 * i + h + 1) * P], src[p][:, h * P:(h + 1) * P], ident)
                    mm.then_inc(a_c, 1)

                def scores(t, p):
                    wait(pe, a_qkT, t + 1)
                    wait(pe, a_st, t)
                    for h in range(NH):
                        pe.matmul(ps[:, 2, h * P:(h + 1) * P], QKT[p][:, 2 + h, :], QKT[p][:, h, :], start=True, stop=True)

                def kv(t, p):
                    wait(pe, a_kr, t + 1)
                    wait(pe, a_v, t + 1)
                    for h in range(NH):
                        for c in range(2):
                            r = slice(c * CH, (c + 1) * CH)
                            mm = pe.matmul(kv_bank(h, c), KR[p][r, h * P:(h + 1) * P],
                                           Va[p][r, h * P:(h + 1) * P], start=True, stop=True)
                    mm.then_inc(a_kv, 1)

                def outputs(t, p):
                    wait(pe, a_sm, t + 1)
                    wait(pe, a_s1, t + 1)
                    wait(pe, a_ow, t)
                    for h in range(NH):
                        pe.matmul(ps[:, 1, h * P:(h + 1) * P], Va[p][:, h * P:(h + 1) * P], SM[p][:, h * P:(h + 1) * P],
                                  start=True, stop=False, skip_group_check=True)
                        for c in range(2):
                            mm = pe.matmul(ps[:, 1, h * P + c * CH:h * P + (c + 1) * CH], ST[2 * p + c][:, h, :],
                                           QKT[p][:, h, c * CH:(c + 1) * CH], start=False, stop=c == 1, skip_group_check=True)
                    mm.then_inc(a_o, 1)

                def step(t, p):
                    project(t, p)
                    first_tile = isinstance(t, int) and t == 0
                    if not first_tile:
                        turn_qk(t - 1, 1 - p)
                        scores(t - 1, 1 - p)
                        kv(t - 1, 1 - p)
                    sums(t, p)
                    if not first_tile:
                        outputs(t - 1, 1 - p)

                def turn(m):
                    for p in range(2):
                        step(2 * m + p, p)
                turn(0)
                with pe.Fori(1, NT // 2) as m:
                    turn(m)
                turn_qk(NT - 1, 1)
                scores(NT - 1, 1)
                kv(NT - 1, 1)
                outputs(NT - 1, 1)
                for h in range(2):
                    pe.wait_ge(f_sq, h + 1)
                    for k in range(NH):
                        mm = pe.matmul(ps[:, 4 + h, :], ones, Sq[h][:, k, :], start=k == 0, stop=k == NH - 1)
                    mm.then_inc(f_ss, 1)
                pe.wait_ge(a_wo, 1)
                pe.wait_ge(a_st, NT)
                for h in range(2):
                    for d in range(KD):
                        for k in range(NH):
                            mm = pe.matmul(ps[:, (6 if h == 0 else 2) + d, :], WO[:, k, d * P:(d + 1) * P], OT[:, k, half(h)],
                                           start=k == 0, stop=k == NH - 1)
                    mm.then_inc(f_y, 1)

            norm_stats(0)
            logits(0)
            ffn(0)
            norm_stats(1)
            attention()
            norm_stats(2)
            logits(1)
            ffn(1)

        @block.scalar
        def _(act):
            def norm_scale(c):
                for h in range(2):
                    act.wait_ge(s_d, 2 * c + h + 1)
                    act.activation(Sq[h], Dv[h][:, :, :], ACT.Square).then_inc(s_sq, 1)
                for h in range(2):
                    act.wait_ge(s_var, 2 * c + h + 1)
                    act.activation(Lv[h], ps[:, 6 + h, :], ACT.Ln, bias=eps_ln[:, :]).then_inc(s_ln, 1)
                    act.wait_ge(s_ln, 2 * c + h + 1)
                    act.activation(Rs[h], Lv[h], ACT.Exp, scale=-0.5).then_inc(s_rs, 1)

            def split_x(f):
                for h in range(2):
                    act.wait_ge(s_xn, 4 * f + h + 1)
                    act.activation(XH[:, :, half(h)], XN[:, :, half(h)], ACT.Copy).then_inc(s_xh, 1)

            def split_w(f, j, p):
                if f == 0:
                    act.wait_ge(s_wr[p], 16 * (j // 2 + 1) if isinstance(j, int) else 8 * (j - p) + 16)
                wait(act, s_l2, UNITS * f + 2 * j - 2)
                act.activation(WH[p][:, :], WR[:, bass.ds(j, 1), :].rearrange("p a n -> p (a n)"), ACT.Copy).then_inc(s_wh, 1)

            def router(f):
                act.wait_ge(s_lgc, f + 1)
                act.activation(pe_[:, :, :], lg[:, :, :], ACT.Exp).then_inc(s_ex, 1)
                sgate = ps[:, 0, 0:NT * NC].rearrange("p (t c) -> p t c", c=NC)[:, :, NE]
                act.activation(sgt[:, :], sgate, ACT.Exp, scale=-1.0).then_inc(s_sgx, 1)

            def ffn(f):
                def silu(u, h):
                    wait(act, s_g, UNITS * f + u + 1)
                    wait(act, s_tc, UNITS * f + u - 1)
                    act.activation(Sg[h], ps[:, 4 + h, :], ACT.Silu).then_inc(s_si, 1)

                def high(u, h):
                    wait(act, s_h, UNITS * f + u + 1)
                    wait(act, s_l2, UNITS * f + u - 1)
                    act.activation(HH[h][:, :], Hf[h], ACT.Copy).then_inc(s_hh, 1)

                def turn(m):
                    for k in range(4):
                        silu(4 * m + k, k % 2)
                        if isinstance(m, int) and m == 0 and k == 0:
                            act.wait_ge(s_ct, f + 1)
                            act.activation(cT[:, :], ps[0:NC, 1:3, :], ACT.Copy).then_inc(s_cts, 1)
                        high(4 * m + k, k % 2)
                        if k == 0 and not (isinstance(m, int) and m == 0):
                            split_w(f, 2 * m + 1, 1)
                        if k == 2 and not (isinstance(m, int) and m == NM - 1):
                            split_w(f, 2 * m + 2, 0)
                turns(act, turn, NM - 1)

            def attention():
                def gates(t, p):
                    wait(act, a_kq, t + 1)
                    wait(act, a_a, t)
                    act.activation(Ea, ps[:, 4, :], ACT.Exp, scale=-1.0).then_inc(a_e, 1)
                    wait(act, a_z, t + 1)
                    wait(act, a_o, t - 1)
                    act.activation(Va[p], ps[:, 5, 0:D], ACT.Copy).then_inc(a_v, 1)

                def logs(t, p):
                    wait(act, a_r, t + 1)
                    act.activation(Ga, Ra[p][:, 0:D], ACT.Exp, scale=-1.0).then_inc(a_g, 1)
                    wait(act, a_g, t + 1)
                    wait(act, a_b, t - 1)
                    act.activation(La[p], Ga, ACT.Ln, bias=one[:, :]).then_inc(a_L, 1)
                    wait(act, a_L, t + 1)
                    wait(act, a_k, t - 1)
                    act.activation(Xa[p], La[p], ACT.Exp, scale=-1.0).then_inc(a_ex, 1)

                def decays(t, p):
                    wait(act, a_b, t + 1)
                    wait(act, a_qk, t - 1)
                    wait(act, a_kr, t - 1)
                    wait(act, a_st, t - 1)
                    act.activation(E2[p], ps[:, 6, 0:D], ACT.Exp)
                    act.activation(E13[p], ps[:, 6, :], ACT.Exp, scale=-1.0)
                    act.activation(DC[p][:, :, :], ps[:, 0, 0:4].rearrange("p (h c) -> p h c", h=NH), ACT.Exp,
                                   scale=-1.0).then_inc(a_e3, 1)

                def turned(t, p):
                    wait(act, a_c, t + 1)
                    wait(act, a_o, t - 1)
                    act.activation(QKT[p], ps[:, 3, :].rearrange("p (i n) -> p i n", i=4), ACT.Copy).then_inc(a_qkT, 1)

                def outputs(t):
                    wait(act, a_o, t + 1)
                    o = ps[:, 1, 0:NH * P].rearrange("p (h n) -> p h n", h=NH)
                    act.activation(OT[:, :, bass.ts(t, P)], o, ACT.Copy).then_inc(a_ow, 1)

                def step(t, p):
                    gates(t, p)
                    first_tile = isinstance(t, int) and t == 0
                    if not first_tile:
                        turned(t - 1, 1 - p)
                    logs(t, p)
                    decays(t, p)
                    if not first_tile:
                        outputs(t - 1)

                def turn(m):
                    for p in range(2):
                        step(2 * m + p, p)
                turn(0)
                with act.Fori(1, NT // 2) as m:
                    turn(m)
                turned(NT - 1, 1)
                outputs(NT - 1)
                for h in range(2):
                    act.wait_ge(a_ow, NT // 2 * (h + 1))
                    act.activation(Sq[h], OT[:, :, half(h)], ACT.Square).then_inc(f_sq, 1)
                for h in range(2):
                    act.wait_ge(f_ss, h + 1)
                    act.activation(Lv[h], ps[:, 4 + h, :], ACT.Ln, bias=eps_rms[:, :]).then_inc(f_ln, 1)
                    act.wait_ge(f_ln, h + 1)
                    act.activation(Rs[h], Lv[h], ACT.Exp, scale=-0.5).then_inc(f_r, 1)

            act.wait_ge(s_set, 1)
            norm_scale(0)
            split_x(0)
            split_w(0, 0, 0)
            split_w(0, 1, 1)
            router(0)
            ffn(0)
            norm_scale(1)
            attention()
            norm_scale(2)
            split_x(1)
            split_w(1, 0, 0)
            split_w(1, 1, 1)
            router(1)
            ffn(1)

        @block.gpsimd
        def _(pool):
            def ffn(f):
                def weigh(u, m, p, h):
                    wait(pool, s_si, UNITS * f + u + 1)
                    if h == 0:
                        wait(pool, s_cb[p], 16 * (NM * f + m + 1))
                    wait(pool, s_h, UNITS * f + u - 1)
                    pool.tensor_tensor(Tc[h], Sg[h], CB[p][:, half(h)], ALU.mult).then_inc(s_tc, 1)

                def turn(m):
                    for k in range(4):
                        weigh(4 * m + k, m, k // 2, k % 2)
                turns(pool, turn, NM - 1)

            def attention():
                def stage(t, p):
                    if isinstance(t, int) and t < 2:
                        pool.wait_ge(s_xn, 4)
                    wait(pool, a_z, t - 1)
                    pool.tensor_copy(XT[p][:, :, :], XN[:, :, bass.ts(t, P)]).then_inc(a_xt, 1)

                def k_rem(t, p):
                    wait(pool, a_k, t + 1)
                    wait(pool, a_e3, t + 1)
                    wait(pool, a_kv, t - 1)
                    pool.tensor_tensor(KR[p], Ka[p], E13[p][:, D:2 * D], ALU.mult).then_inc(a_kr, 1)

                def turn(m):
                    for p in range(2):
                        if not (isinstance(m, int) and m == NT // 2 - 1 and p == 1):
                            stage(2 * m + p + 1, 1 - p)
                        k_rem(2 * m + p, p)
                stage(0, 0)
                turns(pool, turn, NT // 2 - 1)

            ffn(0)
            attention()
            ffn(1)

        @block.vector
        def _(dve):
            chain = [0]

            def link(ins):
                chain[0] += 1
                ins.then_inc(s_chain, 1)
                dve.wait_ge(s_chain, chain[0])

            def over_k(a):
                return spread(a, 1, KD)

            def norm(c):
                for h in range(2):
                    dve.wait_ge(s_mean, 2 * c + h + 1)
                    dve.tensor_tensor(Dv[h][:, :, :], X[:, :, half(h)], over_k(ps[:, 4 + h, :]), ALU.subtract).then_inc(s_d, 1)
                for h in range(2):
                    dve.wait_ge(s_rs, 2 * c + h + 1)
                    dve.wait_ge(s_d, 2 * c + h + 1)
                    dve.tensor_tensor(XN[:, :, half(h)], Dv[h][:, :, :], over_k(Rs[h]), ALU.mult).then_inc(s_xn, 1)

            def split_x(f):
                for h in range(2):
                    dve.wait_ge(s_xh, 2 * f + h + 1)
                    dve.tensor_tensor(XL[:, :, half(h)], XN[:, :, half(h)], XH[:, :, half(h)].bitcast(F32),
                                      ALU.subtract).then_inc(s_xl, 1)

            def split_w(f, j, p):
                wait(dve, s_wh, NJ * f + j + 1)
                dve.tensor_tensor(WL[p][:, :], WR[:, bass.ds(j, 1), :].rearrange("p a n -> p (a n)"),
                                  WH[p][:, :].bitcast(F32), ALU.subtract).then_inc(s_wl, 1)

            def experts(a):
                return spread(a, 2, NE)

            def router(f):
                dve.wait_ge(s_lg, f + 1)
                logit = ps[:, 0, 0:NT * NC].rearrange("p (t c) -> p t c", c=NC)[:, :, 0:NE]
                link(dve.tensor_reduce(t1[:, :], logit, AX.X, ALU.max))
                dve.tensor_tensor(lg[:, :, :], logit, experts(t1[:, :]), ALU.subtract).then_inc(s_lgc, 1)
                dve.wait_ge(s_ex, f + 1)
                link(dve.tensor_reduce(t1[:, :], pe_[:, :, :], AX.X, ALU.add))
                link(dve.reciprocal(t2[:, :], t1[:, :]))
                link(dve.tensor_tensor(pr[:, :, :], pe_[:, :, :], experts(t2[:, :]), ALU.mult))
                for t in range(NT - 1):
                    dve.max(m8[:, t, :], pr[:, t, :])
                link(dve.max(m8[:, NT - 1, :], pr[:, NT - 1, :]))
                kth = experts(m8[:, :, TOPK - 1])
                dve.tensor_tensor(gt[:, :, :], pr[:, :, :], kth, ALU.is_gt)
                link(dve.tensor_tensor(eq[:, :, :], pr[:, :, :], kth, ALU.is_equal))
                dve.tensor_reduce(t1[:, :], gt[:, :, :], AX.X, ALU.add)
                link(dve.tensor_copy(cs[0][:, :, NE:2 * NE], eq[:, :, :]))
                a = 0
                for shift in (1, 2, 4, 8):
                    link(dve.tensor_tensor(cs[1 - a][:, :, NE:2 * NE], cs[a][:, :, NE:2 * NE],
                                           cs[a][:, :, NE - shift:2 * NE - shift], ALU.add))
                    a = 1 - a
                link(dve.tensor_tensor(lg[:, :, :], cs[a][:, :, NE:2 * NE], experts(t1[:, :]), ALU.add))
                link(dve.scalar_tensor_tensor(pe_[:, :, :], lg[:, :, :], float(TOPK), eq[:, :, :], ALU.is_le, ALU.mult))
                link(dve.tensor_tensor(gt[:, :, :], gt[:, :, :], pe_[:, :, :], ALU.add))
                dve.tensor_tensor(cf[:, :, 0:NE], pr[:, :, :], gt[:, :, :], ALU.mult)
                dve.wait_ge(s_sgx, f + 1)
                link(dve.tensor_scalar(t2[:, :], sgt[:, :], 1.0, None, ALU.add))
                dve.reciprocal(cf[:, :, NE], t2[:, :]).then_inc(s_coef, 1)

            def ffn(f):
                def hidden(u, h):
                    wait(dve, s_tc, UNITS * f + u + 1)
                    wait(dve, s_u, UNITS * f + u + 1)
                    wait(dve, s_hl, UNITS * f + u - 1)
                    dve.tensor_tensor(Hf[h], ps[:, 6 + h, :], Tc[h], ALU.mult).then_inc(s_h, 1)

                def low(u, h):
                    wait(dve, s_hh, UNITS * f + u + 1)
                    dve.tensor_tensor(HL[h][:, :], Hf[h], HH[h][:, :].bitcast(F32), ALU.subtract).then_inc(s_hl, 1)

                def turn(m):
                    for k in range(4):
                        hidden(4 * m + k, k % 2)
                        low(4 * m + k, k % 2)
                        if k == 0 and not (isinstance(m, int) and m == 0):
                            split_w(f, 2 * m + 1, 1)
                        if k == 2 and not (isinstance(m, int) and m == NM - 1):
                            split_w(f, 2 * m + 2, 0)
                turns(dve, turn, NM - 1)
                dve.wait_ge(s_l2, UNITS * (f + 1))
                for h in range(2):
                    dve.scalar_tensor_tensor(X[:, :, half(h)], ps[:, 2 * h:2 * h + 2, :], 0.5, X[:, :, half(h)],
                                             ALU.mult, ALU.add).then_inc(s_xr, 1)

            def attention():
                for k in range(NH):
                    if k == 0:
                        dve.wait_ge(s_wa, 48)
                    ins = dve.tensor_scalar(WO[:, k, :], WO[:, k, :], nw[:, k:k + 1], None, ALU.mult)
                ins.then_inc(a_wo, 1)

                def sigmoids(t, p):
                    wait(dve, a_e, t + 1)
                    dve.tensor_scalar(Aa, Ea, 1.0, None, ALU.add).then_inc(a_a, 1)
                    wait(dve, a_a, t + 1)
                    wait(dve, a_g, t - 1)
                    dve.reciprocal(Ra[p], Aa).then_inc(a_r, 1)
                    wait(dve, a_r, t + 1)
                    dve.tensor_tensor(Qa[p], ps[:, 4, D:2 * D], Ra[p][:, D:2 * D], ALU.mult).then_inc(a_q, 1)

                def decayed(t, p):
                    wait(dve, a_ex, t + 1)
                    wait(dve, a_kr, t - 1)
                    dve.tensor_scalar(Ka[p], Xa[p], -1.0, 1.0, ALU.mult, ALU.add).then_inc(a_k, 1)
                    wait(dve, a_k, t + 1)
                    wait(dve, a_e3, t + 1)
                    wait(dve, a_c, t - 1)
                    dve.tensor_tensor(QD[p], Qa[p], E13[p][:, 0:D], ALU.mult)
                    dve.tensor_tensor(KD_[p], Ka[p], E2[p], ALU.mult).then_inc(a_qk, 1)

                def states(t, p):
                    wait(dve, a_st, t)
                    wait(dve, a_o, t - 1)
                    wait(dve, a_kv, t + 1)
                    for c in range(2):
                        if c == 1:
                            dve.copy_predicated(SM[p][:, :], tri2, ps[:, 2, 0:NH * P]).then_inc(a_sm, 1)
                            wait(dve, a_s1, t + 1)
                            wait(dve, a_o, t)
                        to = ST[(2 * p + c + 1) % 4]
                        for h in range(NH):
                            ins = dve.scalar_tensor_tensor(to[:, h, :], ST[2 * p + c][:, h, :], DC[p][:, h, c:c + 1],
                                                           kv_bank(h, c), ALU.mult, ALU.add)
                        ins.then_inc((a_s1, a_st)[c], 1)

                def step(t, p):
                    sigmoids(t, p)
                    first_tile = isinstance(t, int) and t == 0
                    if not first_tile:
                        states(t - 1, 1 - p)
                    decayed(t, p)

                def turn(m):
                    for p in range(2):
                        step(2 * m + p, p)
                turn(0)
                with dve.Fori(1, NT // 2) as m:
                    turn(m)
                states(NT - 1, 1)
                for h in range(2):
                    dve.wait_ge(f_y, h + 1)
                    dve.wait_ge(f_r, h + 1)
                    b = 6 if h == 0 else 2
                    dve.tensor_tensor(Dv[h][:, :, :], ps[:, b:b + 2, :], over_k(Rs[h]), ALU.mult).then_inc(f_t, 1)
                    dve.wait_ge(f_t, h + 1)
                    dve.tensor_tensor(X[:, :, half(h)], X[:, :, half(h)], Dv[h][:, :, :], ALU.add).then_inc(s_xr, 1)

            dve.memset(eps_ln[:, :], LN_EPS)
            dve.memset(eps_rms[:, :], RMS_EPS)
            dve.memset(one[:, :], 1.0).then_inc(s_set, 1)
            for a in range(2):
                dve.memset(cs[a][:, :, 0:NE], 0.0)
                dve.memset(SM[a][:, :], 0.0)
            link(dve.memset(ST[0][:, :, :], 0.0))
            norm(0)
            split_x(0)
            split_w(0, 0, 0)
            split_w(0, 1, 1)
            router(0)
            ffn(0)
            norm(1)
            attention()
            norm(2)
            split_x(1)
            split_w(1, 0, 0)
            split_w(1, 1, 1)
            router(1)
            ffn(1)


def layout(inputs):
    a = {k: np.asarray(v) for k, v in inputs.items()}

    def tiles(w):
        return np.ascontiguousarray(w.reshape(-1, P, w.shape[1]).transpose(1, 0, 2))

    w13, w2 = a["L0_ffn_w13"], a["L0_ffn_w2"]
    sgu, sd = a["L0_ffn_shared_gate_up_w"], a["L0_ffn_shared_down_w"]
    pad = np.zeros((NJ * P - NE * FE - FS, D), w13.dtype)
    gate = np.concatenate([w13[:, :FE].reshape(-1, D), sgu[:FS], pad])
    up = np.concatenate([w13[:, FE:].reshape(-1, D), sgu[FS:], pad])
    down = np.concatenate([w2.transpose(0, 2, 1).reshape(-1, D), sd.T, pad])
    w = np.empty((NJ, P, WC), w13.dtype)
    for i, m in enumerate((gate, up)):
        part = m.reshape(NJ, P, KD, P).transpose(0, 3, 2, 1)
        w[:, :, i * KD * P:(i + 1) * KD * P] = part.reshape(NJ, P, KD * P)
    w[:, :, 2 * KD * P:] = down.reshape(NJ, P, D)

    s, t = np.arange(P)[:, None], np.arange(P)[None, :]
    same = s // CH == t // CH
    tri = (same & (s <= t)).astype(np.float32)
    c = np.zeros((P, C_ALL), np.float32)
    c[:, C_ONES:C_ONES + P] = 1.0 / D
    c[:, C_ID:C_ID + P] = np.eye(P)
    c[:, C_TRI:C_TRI + P] = tri
    c[:, C_TRI + P:C_TRI + 2 * P] = tri
    c[:, C_REM:C_REM + P] = same & (s > t)
    c[:, C_CHUNK:C_CHUNK + 2] = s // CH == np.arange(2)[None, :]
    return {
        "xT": tiles(a["L0_attn_x"][0].T),
        "wffn": w,
        "wgate": tiles(np.concatenate([a["L0_ffn_gate_w"], a["L0_ffn_sgate_w"]]).T),
        "wkqv": tiles(np.concatenate([a["L0_attn_Wk"], a["L0_attn_Wq"], a["L0_attn_Wv"]]).T),
        "woT": tiles(a["L0_attn_Wo"].T),
        "normw": np.ascontiguousarray(a["L0_attn_norm_w"].reshape(NH, P).T),
        "consts": c,
    }


def kernel(**inputs):
    import concourse.bacc as bacc
    from concourse.bass_utils import run_bass_kernel_spmd

    nc = bacc.Bacc("TRN2", target_bir_lowering=False, num_devices=1)
    arrays = layout(inputs)
    args = [nc.dram_tensor(k, v.shape, mybir.dt.from_np(v.dtype), kind="ExternalInput").ap() for k, v in arrays.items()]
    out = nc.dram_tensor("out_t", (P, KD, N), F32, kind="ExternalOutput").ap()
    macaron(nc, *args, out)
    r = run_bass_kernel_spmd(nc, [arrays], core_ids=[0])
    y = r.results[0]["out_t"]
    return np.ascontiguousarray(y.transpose(2, 1, 0).reshape(1, N, D))
```

```python
from contextlib import ExitStack

import numpy as np

import concourse.bass as bass
from concourse import mybir

F32 = mybir.dt.float32
F32R = mybir.dt.float32r
I32 = mybir.dt.int32
ALU = mybir.AluOpType
ACT = mybir.ActivationFunctionType
AX = mybir.AxisListType

P = 128
N = 1024
D = 256
KD = D // P
HALF = 512
NE, TOPK = 16, 4
FE, FS = 176, 704
GRP = 16
NJ = -(-(NE * FE + FS) // P)
NG = NJ * P // GRP
WC = 2 * KD * P + D
NC = NE + 1
NT = N // P
CH = 64
NH = 2
LN_EPS, RMS_EPS = 1e-5, 1e-6
UNITS = 2 * NJ
TURN = 8
NM = UNITS // TURN
LAG = 7
SPLIT = LAG - 1
RUN = 8
NQ, QUART = 4, N // 4

C_ID, C_TRI, C_REM, C_CHUNK = 0, 128, 384, 512
C_ALL = 514


def spread(a, axis, n):
    a = a.unsqueeze(axis)
    shape = list(a.shape)
    shape[axis] = n
    return a.broadcast_to(shape)


def macaron(nc, xT, wffn, wgate, wkqv, woT, normw, consts, out):
    ctx = ExitStack()

    def sb(name, shape, dt=F32):
        return ctx.enter_context(nc.sbuf_tensor(name, shape, dt))

    def sem(name):
        return ctx.enter_context(nc.semaphore(name))

    with ctx:
        ps = ctx.enter_context(nc.psum_tensor("ps", [P, 8, HALF], F32))
        coef_dram = nc.dram_tensor("coef_groups", [NG, N], F32, kind="Internal").ap()
        cst = sb("cst", [P, C_ALL])
        X = sb("X", [P, KD, N])
        XN = sb("XN", [P, KD, N])
        XH = sb("XH", [P, KD, N], F32R)
        XL = sb("XL", [P, KD, N], F32R)
        WR = sb("WR", [P, NJ, WC])
        WH = [sb(f"WH{p}", [P, WC], F32R) for p in range(2)]
        WL = [sb(f"WL{p}", [P, WC], F32R) for p in range(2)]
        WG = sb("WG", [P, KD, NC])
        WA = sb("WA", [P, KD, 3 * D])
        WO = sb("WO", [P, NH, D])
        nw = sb("nw", [P, NH])
        eps_ln = sb("eps_ln", [P, 1])
        eps_rms = sb("eps_rms", [P, 1])
        one = sb("one", [P, 1])
        zeros = sb("zeros", [P, HALF], mybir.dt.bfloat16)
        mean_of = sb("mean_of", [P, P])
        ar = sb("ar", [P, 15 * HALF])

        def area(at, n):
            return ar[:, at:at + n]

        Dv = sb("Dv", [P, NQ, KD, QUART])
        Sq = [area(q * HALF, HALF).rearrange("p (k n) -> p k n", k=KD) for q in range(NQ)]
        Lv = [area(4 * HALF + q * QUART, QUART) for q in range(NQ)]
        Rs = [area(6 * HALF + q * QUART, QUART) for q in range(NQ)]
        CB = [area(2 * p * HALF, N) for p in range(2)]
        Sg = [area((4 + h) * HALF, HALF) for h in range(2)]
        Hu = [area((6 + i) * HALF, HALF) for i in range(TURN)]
        Hf = [Dv[:, h, :, :].rearrange("p k n -> p (k n)") for h in range(2)]
        HH = [sb(f"HH{h}", [P, HALF], F32R) for h in range(2)]
        HL = [sb(f"HL{h}", [P, HALF], F32R) for h in range(2)]
        lg = sb("lg", [P, NT, NE])
        pe_ = sb("pe_", [P, NT, NE])
        pr = sb("pr", [P, NT, NE])
        m8 = sb("m8", [P, NT, 8])
        t1 = sb("t1", [P, NT])
        t2 = sb("t2", [P, NT])
        sgt = sb("sgt", [P, NT])
        gt = sb("gt", [P, NT, NE])
        eq = sb("eq", [P, NT, NE])
        cs = [sb(f"cs{i}", [P, NT, 2 * NE]) for i in range(2)]
        cf = sb("cf", [P, NT, NC])
        cT = sb("cT", [NC, N])
        GQ = area(0, 8 * HALF).rearrange("p (t n) -> p t n", t=NT)
        VV = area(8 * HALF, 4 * HALF).rearrange("p (t n) -> p t n", t=NT)
        E13 = [area((12 + p) * HALF, HALF) for p in range(2)]
        E2 = [area(14 * HALF + p * D, D) for p in range(2)]
        Ga = sb("Ga", [P, D])
        Ka = [sb(f"Ka{p}", [P, D]) for p in range(2)]
        QKT = [Dv[:, p, :, :].rearrange("p k (i n) -> p (k i) n", n=P) for p in range(2)]
        Va = [Dv[:, 2, p, :] for p in range(2)]
        La = [Dv[:, 3, p, :] for p in range(2)]
        DC = [sb(f"DC{p}", [P, NH, 2]) for p in range(2)]
        SM = [sb(f"SM{p}", [P, NH * P]) for p in range(2)]
        ST = [sb(f"ST{i}", [P, NH, P]) for i in range(4)]
        OT = XN
        Os = [area(h * N, N).rearrange("p (k n) -> p k n", k=NH) for h in range(2)]
        Ol = [area((8 + h) * HALF, HALF) for h in range(2)]
        Or = [area((10 + h) * HALF, HALF) for h in range(2)]

        ident = cst[:, C_ID:C_ID + P]
        tri = cst[:, C_TRI:C_TRI + P]
        tri2 = cst[:, C_TRI:C_TRI + NH * P].bitcast(I32)
        rem = cst[:, C_REM:C_REM + P]
        chunk = cst[:, C_CHUNK:C_CHUNK + 2]

        s_xin = [sem(f"s_xin{q}") for q in range(NQ)]
        s_cst, s_wg, s_wa, s_out, s_cg = (sem(n) for n in ("s_cst", "s_wg", "s_wa", "s_out", "s_cg"))
        s_wr = [sem(f"s_wr{p}") for p in range(2)]
        s_cb = [sem(f"s_cb{p}") for p in range(2)]
        s_set = sem("s_set")
        s_mean, s_d, s_sq, s_var, s_ln, s_rs, s_xn, s_xh, s_xl, s_xr = (
            sem(n) for n in "s_mean s_d s_sq s_var s_ln s_rs s_xn s_xh s_xl s_xr".split())
        s_lg, s_lgc, s_ex, s_sgx, s_coef, s_ct, s_cts, s_chain = (
            sem(n) for n in "s_lg s_lgc s_ex s_sgx s_coef s_ct s_cts s_chain".split())
        s_w1h, s_w1l, s_w2h, s_w2l, s_g, s_u, s_si, s_hu, s_tc, s_hh, s_hl, s_l2 = (
            sem(n) for n in "s_w1h s_w1l s_w2h s_w2l s_g s_u s_si s_hu s_tc s_hh s_hl s_l2".split())
        a_wh, a_wl, a_kq, a_z, a_sg, a_v, a_q, a_g, a_L, a_ex, a_b, a_e3, a_k, a_qk, a_kr, a_va, a_c, a_qkT, a_kv, a_sm, \
            a_s1, a_st, a_o, a_ow, a_wo = (sem("a_" + n) for n in (
                "wh wl kq z sg v q g L ex b e3 k qk kr va c qkT kv sm s1 st o ow wo").split())
        f_sq, f_ss, f_ln, f_r, f_y, f_t = (sem("f_" + n) for n in "sq ss ln r y t".split())

        block = ctx.enter_context(nc.Block())

        def wait(eng, s, v):
            if isinstance(v, int) and v <= 0:
                return
            eng.wait_ge(s, v)

        def half(h):
            return slice(h * HALF, (h + 1) * HALF)

        def quarter(q):
            return slice(q * QUART, (q + 1) * QUART)

        def static(x, value=None):
            return isinstance(x, int) and value in (None, x)

        W1, W2 = slice(0, 2 * KD * P), slice(2 * KD * P, WC)

        def kv_bank(h, c):
            return ps[:, 2, (NH + h) * P:(NH + h + 1) * P] if c == 0 else ps[:, 7, h * P:(h + 1) * P]

        def turns(eng, body, last):
            body(0)
            with eng.Fori(1, last) as m:
                body(m)
            body(last)

        def ffn_turn(f, m, k, split_h, split_w1, split_w2):
            if k % 2 == 0 and not (static(m, NM - 1) and k == TURN - 2):
                split_w1(f, TURN // 2 * m + k // 2 + 1, (k // 2 + 1) % 2)
            if not static(m, 0) or k >= SPLIT:
                split_h(TURN * m + k - SPLIT, k % 2)
            if k % 2 == 1 and (not static(m, 0) or k >= SPLIT - 1):
                j = (k - SPLIT + 1) // 2
                split_w2(f, TURN // 2 * m + j, j % 2)

        def ffn_tail(f, split_h, split_w2):
            for k in range(SPLIT):
                split_h(UNITS + k - SPLIT, k % 2)
                if k % 2 == 1 and k < SPLIT - 1:
                    j = NJ + (k - SPLIT + 1) // 2
                    split_w2(f, j, j % 2)

        @block.sync
        def _(sp):
            def load_w(j, p):
                sp.dma_start(WR[:, bass.ds(j, 1), :], wffn[bass.ds(j, 1), :, :].rearrange("a p n -> p a n")).then_inc(s_wr[p], 16)

            def load_cb(j, p):
                src = coef_dram[bass.ds(j * (P // GRP), P // GRP), :]
                sp.dma_start(CB[p], spread(src, 1, GRP)).then_inc(s_cb[p], 16)

            for q in range(NQ):
                sp.dma_start(X[:, :, quarter(q)], xT[:, :, quarter(q)]).then_inc(s_xin[q], 16)
            sp.dma_start(WG[:, :, :], wgate).then_inc(s_wg, 16)
            for j in range(RUN):
                if j >= 2:
                    sp.wait_ge(s_wr[j % 2], 16 * (j // 2))
                load_w(j, j % 2)
                if j == 1:
                    sp.dma_start(cst[:, :], consts).then_inc(s_cst, 16)
            sp.dma_start(WA[:, :, :], wkqv).then_inc(s_wa, 16)
            sp.dma_start(WO[:, :, :], woT).then_inc(s_wa, 16)
            sp.dma_start(nw[:, :], normw).then_inc(s_wa, 16)

            for f in range(2):
                sp.wait_ge(s_cts, f + 1)
                er = NE * (FE // GRP)
                rows = coef_dram[0:er, :].rearrange("(e r) n -> e r n", r=FE // GRP)
                sp.dma_start(rows, spread(cT[0:NE, :], 1, FE // GRP)).then_inc(s_cg, 16)
                sp.dma_start(coef_dram[er:NG, :].rearrange("(a r) n -> a r n", a=1),
                             spread(cT[NE:NC, :], 1, NG - er)).then_inc(s_cg, 16)
                sp.wait_ge(s_cg, 32 * (f + 1))
                for p in range(2):
                    load_cb(p, p)

                def turn(m, weights, slices=TURN // 2):
                    for k in range(slices):
                        p = k % 2
                        if weights:
                            sp.wait_ge(s_wr[p], 16 * (m * (TURN // 4) + (k + RUN) // 2))
                            load_w(m * (TURN // 2) + k + RUN, p)
                        sp.wait_ge(s_tc, UNITS * f + TURN * m + 2 * k + 2)
                        load_cb(m * (TURN // 2) + k + 2, p)

                if f == 0:
                    with sp.Fori(0, NM - 2) as m:
                        turn(m, True)
                    turn(NM - 2, False)
                else:
                    with sp.Fori(0, NM - 1) as m:
                        turn(m, False)
                turn(NM - 1, False, TURN // 2 - 2)

            for q in range(NQ):
                sp.wait_ge(s_xr, 2 * NQ + q + 1)
                sp.dma_start(out[:, :, quarter(q)], X[:, :, quarter(q)]).then_inc(s_out, 16)
            sp.wait_ge(s_out, 16 * NQ)

        @block.tensor
        def _(pe):
            def norm_stats(c):
                def stat(q, of_squares):
                    for k in range(KD):
                        x = Sq[q][:, k, :] if of_squares else X[:, k, quarter(q)]
                        mm = pe.matmul(ps[:, 4 + q, 0:QUART], mean_of[:, :], x, start=k == 0, stop=k == KD - 1)
                    mm.then_inc(s_var if of_squares else s_mean, 1)

                def mean(q):
                    if c == 0:
                        pe.wait_ge(s_xin[q], 16)
                    else:
                        pe.wait_ge(s_xr, NQ * (c - 1) + q + 1)
                    stat(q, False)

                def var(q):
                    pe.wait_ge(s_sq, NQ * c + q + 1)
                    stat(q, True)

                if c == 0:
                    pe.wait_ge(s_set, 1)
                if c == 2:
                    pe.wait_ge(f_t, 2)
                mean(0)
                for q in range(1, NQ):
                    mean(q)
                    var(q - 1)
                var(NQ - 1)

            def logits(f):
                if f == 0:
                    pe.wait_ge(s_wg, 16)
                for t in range(NT):
                    pe.wait_ge(s_xn, 2 * NQ * f + t * P // QUART + 1)
                    for k in range(KD):
                        mm = pe.matmul(ps[:, 0, t * NC:(t + 1) * NC], XN[:, k, t * P:(t + 1) * P], WG[:, k, :],
                                       start=k == 0, stop=k == KD - 1)
                mm.then_inc(s_lg, 1)

            def turn_coefs(f):
                if f == 0:
                    pe.wait_ge(s_cst, 16)
                pe.wait_ge(s_coef, f + 1)
                for t in range(NT):
                    mm = pe.transpose(ps[0:NC, 1 + t // 4, (t % 4) * P:(t % 4 + 1) * P], cf[:, t, :], ident)
                mm.then_inc(s_ct, 1)

            def clear(f):
                pe.wait_ge(s_cts, f + 1)
                for bank in range(4):
                    pe.matmul(ps[:, bank, :], zeros[:, 0:P], zeros[:, :], start=True, stop=False, skip_group_check=True)

            def first(f, u, j, p, h):
                if static(u) and u < 2:
                    pe.wait_ge(s_xl, (2 * f * NQ) + (h + 1) * HALF // QUART)
                if h == 0:
                    wait(pe, s_w1l, NJ * f + j + 1)
                for what, bank, done, freed in ((0, 4, s_g, s_si), (1, 6, s_u, s_hu)):
                    wait(pe, freed, UNITS * f + u - 1)
                    n = 0
                    for w, x in ((WH, XH), (WH, XL), (WL, XH)):
                        for k in range(KD):
                            col = (what * KD + k) * P
                            mm = pe.matmul(ps[:, bank + h, :], w[p][:, col:col + P], x[:, k, half(h)],
                                           start=n == 0, stop=n == 5)
                            n += 1
                    mm.then_inc(done, 1)

            def second(f, u, j, p, h, stop):
                if h == 0:
                    wait(pe, s_w2l, NJ * f + j + 1)
                wait(pe, s_hl, UNITS * f + u + 1)
                n = 0
                for w, x in ((WH, HH), (WH, HL), (WL, HH)):
                    for k in range(KD):
                        col = 2 * KD * P + k * P
                        mm = pe.matmul(ps[:, 2 * h + k, :], w[p][:, col:col + P], x[h][:, :],
                                       start=False, stop=stop and n >= 4, skip_group_check=True)
                        n += 1
                mm.then_inc(s_l2, 1)

            def ffn(f):
                def late(m, k):
                    second(f, TURN * m + k, TURN // 2 * m + k // 2, k // 2 % 2, k % 2,
                           static(m, NM - 1) and k >= TURN - 2)

                def turn(m):
                    for k in range(TURN):
                        first(f, TURN * m + k, TURN // 2 * m + k // 2, k // 2 % 2, k % 2)
                        if static(m, 0) and k == 2:
                            turn_coefs(f)
                        if static(m, 0) and k == LAG:
                            clear(f)
                        if not static(m, 0) or k >= LAG:
                            late(m, k - LAG)
                turns(pe, turn, NM - 1)
                for k in range(TURN - LAG, TURN):
                    late(NM - 1, k)

            def attention():
                pe.wait_ge(a_wl, KD)
                for t in range(NT):
                    p, q = t % 2, t * P // QUART
                    tile = slice(t * P, (t + 1) * P)
                    pe.wait_ge(s_xl, 1 * NQ + q + 1)
                    for bank, cols, done, freed in ((0, slice(0, 2 * D), a_kq, a_q), (2, slice(2 * D, 3 * D), a_z, a_v)):
                        wait(pe, freed, t - 1)
                        n = 0
                        for x, w in ((XH, WH), (XL, WH), (XH, WL)):
                            for k in range(KD):
                                mm = pe.matmul(ps[:, bank + p, 0:cols.stop - cols.start], x[:, k, tile], w[k][:, cols],
                                               start=n == 0, stop=n == 5)
                                n += 1
                        mm.then_inc(done, 1)
                pe.wait_ge(a_q, NT)
                pe.wait_ge(a_v, NT)

                def sums(t, p):
                    wait(pe, a_L, t + 1)
                    wait(pe, a_e3, t)
                    pe.matmul(ps[:, 6, 0:D], tri, La[p], start=True, stop=True)
                    pe.matmul(ps[:, 6, D:2 * D], rem, La[p], start=True, stop=True)
                    for h in range(NH):
                        mm = pe.matmul(ps[:, 0, 2 * h:2 * h + 2], La[p][:, h * P:(h + 1) * P], chunk, start=True, stop=True)
                    mm.then_inc(a_b, 1)

                def turn_qk(t, p):
                    wait(pe, a_qk, t + 1)
                    wait(pe, a_qkT, t)
                    for i, src in enumerate((E13, E2)):
                        for h in range(NH):
                            mm = pe.transpose(ps[:, 3, (2 * i + h) * P:(2 * i + h + 1) * P], src[p][:, h * P:(h + 1) * P], ident)
                    mm.then_inc(a_c, 1)

                def scores(t, p):
                    wait(pe, a_qkT, t + 1)
                    wait(pe, a_st, t)
                    for h in range(NH):
                        pe.matmul(ps[:, 2, h * P:(h + 1) * P], QKT[p][:, 2 + h, :], QKT[p][:, h, :], start=True, stop=True)

                def kv(t, p):
                    wait(pe, a_kr, t + 1)
                    wait(pe, a_va, t + 1)
                    for h in range(NH):
                        for c in range(2):
                            r = slice(c * CH, (c + 1) * CH)
                            mm = pe.matmul(kv_bank(h, c), E13[p][r, D + h * P:D + (h + 1) * P],
                                           Va[p][r, h * P:(h + 1) * P], start=True, stop=True)
                    mm.then_inc(a_kv, 1)

                def outputs(t, p):
                    wait(pe, a_sm, t + 1)
                    wait(pe, a_s1, t + 1)
                    wait(pe, a_ow, t)
                    for h in range(NH):
                        pe.matmul(ps[:, 1, h * P:(h + 1) * P], Va[p][:, h * P:(h + 1) * P], SM[p][:, h * P:(h + 1) * P],
                                  start=True, stop=False, skip_group_check=True)
                        for c in range(2):
                            mm = pe.matmul(ps[:, 1, h * P + c * CH:h * P + (c + 1) * CH], ST[2 * p + c][:, h, :],
                                           QKT[p][:, h, c * CH:(c + 1) * CH], start=False, stop=c == 1, skip_group_check=True)
                    mm.then_inc(a_o, 1)

                def step(t, p):
                    if not static(t, NT):
                        sums(t, p)
                    if not static(t, 0):
                        turn_qk(t - 1, 1 - p)
                    if not static(t, 0) and not static(t, 1):
                        outputs(t - 2, p)
                    if not static(t, 0):
                        scores(t - 1, 1 - p)
                        kv(t - 1, 1 - p)

                def turn(m):
                    for p in range(2):
                        step(2 * m + p, p)
                turn(0)
                with pe.Fori(1, NT // 2) as m:
                    turn(m)
                step(NT, 0)
                outputs(NT - 1, 1)

                for h in range(2):
                    pe.wait_ge(f_sq, h + 1)
                    pe.wait_ge(a_e3, NT)
                    for k in range(NH):
                        mm = pe.matmul(ps[:, (6, 0)[h], :], mean_of[:, :], Os[h][:, k, :], start=k == 0, stop=k == NH - 1)
                    mm.then_inc(f_ss, 1)
                pe.wait_ge(a_wo, 1)
                pe.wait_ge(a_st, NT)
                for h in range(2):
                    for d in range(KD):
                        for k in range(NH):
                            mm = pe.matmul(ps[:, (4, 2)[h] + d, :], WO[:, k, d * P:(d + 1) * P], OT[:, k, half(h)],
                                           start=k == 0, stop=k == NH - 1)
                    mm.then_inc(f_y, 1)

            norm_stats(0)
            logits(0)
            ffn(0)
            norm_stats(1)
            attention()
            norm_stats(2)
            logits(1)
            ffn(1)

        @block.scalar
        def _(act):
            def norm_scale(c):
                def square(q):
                    act.wait_ge(s_d, NQ * c + q + 1)
                    act.activation(Sq[q], Dv[:, q, :, :], ACT.Square).then_inc(s_sq, 1)

                def scale(q):
                    act.wait_ge(s_var, NQ * c + q + 1)
                    act.activation(Lv[q], ps[:, 4 + q, 0:QUART], ACT.Ln, bias=eps_ln[:, :]).then_inc(s_ln, 1)
                    act.wait_ge(s_ln, NQ * c + q + 1)
                    act.activation(Rs[q], Lv[q], ACT.Exp, scale=-0.5).then_inc(s_rs, 1)

                def high(q):
                    act.wait_ge(s_xn, NQ * c + q + 1)
                    act.activation(XH[:, :, quarter(q)], XN[:, :, quarter(q)], ACT.Copy).then_inc(s_xh, 1)

                square(0)
                square(1)
                scale(0)
                for q in range(2, NQ):
                    square(q)
                    scale(q - 1)
                    high(q - 2)
                scale(NQ - 1)
                high(NQ - 2)
                high(NQ - 1)

            def split_w(f, j, p, cols, freed, count, done):
                if f == 0:
                    act.wait_ge(s_wr[p], 16 * (j // 2 + 1) if static(j) else 8 * (j - p) + 16)
                wait(act, freed, count)
                w = WR[:, bass.ds(j, 1), cols].rearrange("p a n -> p (a n)")
                act.activation(WH[p][:, cols], w, ACT.Copy).then_inc(done, 1)

            def split_w1(f, j, p):
                split_w(f, j, p, W1, s_u, UNITS * f + 2 * j - 2, s_w1h)

            def split_w2(f, j, p):
                split_w(f, j, p, W2, s_l2, UNITS * f + 2 * j - 2, s_w2h)

            def router(f):
                act.wait_ge(s_lgc, f + 1)
                act.activation(pe_[:, :, :], lg[:, :, :], ACT.Exp).then_inc(s_ex, 1)
                sgate = ps[:, 0, 0:NT * NC].rearrange("p (t c) -> p t c", c=NC)[:, :, NE]
                act.activation(sgt[:, :], sgate, ACT.Exp, scale=-1.0).then_inc(s_sgx, 1)

            def ffn(f):
                def silu(u, h):
                    wait(act, s_g, UNITS * f + u + 1)
                    wait(act, s_hu, UNITS * f + u - 1)
                    act.activation(Sg[h], ps[:, 4 + h, :], ACT.Silu).then_inc(s_si, 1)

                def high(u, h):
                    wait(act, s_tc, UNITS * f + u + 1)
                    wait(act, s_l2, UNITS * f + u - 1)
                    act.activation(HH[h][:, :], Hf[h], ACT.Copy).then_inc(s_hh, 1)

                def turn(m):
                    for k in range(TURN):
                        silu(TURN * m + k, k % 2)
                        if static(m, 0) and k == 2:
                            act.wait_ge(s_ct, f + 1)
                            act.activation(cT[:, :], ps[0:NC, 1:3, :], ACT.Copy).then_inc(s_cts, 1)
                        ffn_turn(f, m, k, high, split_w1, split_w2)
                turns(act, turn, NM - 1)
                ffn_tail(f, high, split_w2)

            def attention():
                for k in range(KD):
                    if k == 0:
                        act.wait_ge(s_l2, UNITS)
                        act.wait_ge(s_wa, 48)
                    act.activation(WH[k][:, :], WA[:, k, :], ACT.Copy).then_inc(a_wh, 1)
                norm_scale(1)
                act.preload_act_table(ACT.Sigmoid)
                for t in range(NT):
                    act.wait_ge(a_kq, t + 1)
                    act.activation(GQ[:, t, :], ps[:, t % 2, :], ACT.Sigmoid).then_inc(a_sg, 1)
                    act.wait_ge(a_z, t + 1)
                    act.activation(VV[:, t, :], ps[:, 2 + t % 2, 0:D], ACT.Copy).then_inc(a_v, 1)
                act.preload_act_table_set("natural_log_exp_and_others")

                def logs(t, p):
                    g = GQ[:, bass.ds(t, 1), 0:D].rearrange("p a n -> p (a n)")
                    if static(t, 0):
                        act.wait_ge(a_sg, NT)
                    act.activation(Ga[:, :], g, ACT.Exp, scale=-1.0).then_inc(a_g, 1)
                    wait(act, a_g, t + 1)
                    wait(act, a_b, t - 1)
                    act.activation(La[p], Ga[:, :], ACT.Ln, bias=one[:, :]).then_inc(a_L, 1)
                    wait(act, a_L, t + 1)
                    wait(act, a_qk, t - 1)
                    wait(act, a_kr, t - 1)
                    act.activation(Ka[p][:, :], La[p], ACT.Exp, scale=-1.0).then_inc(a_ex, 1)

                def decays(t, p):
                    wait(act, a_b, t + 1)
                    wait(act, a_c, t - 1)
                    wait(act, a_kv, t - 1)
                    wait(act, a_st, t - 1)
                    act.activation(E2[p], ps[:, 6, 0:D], ACT.Exp)
                    act.activation(E13[p], ps[:, 6, :], ACT.Exp, scale=-1.0)
                    act.activation(DC[p][:, :, :], ps[:, 0, 0:4].rearrange("p (h c) -> p h c", h=NH), ACT.Exp,
                                   scale=-1.0).then_inc(a_e3, 1)

                def turned(t, p):
                    wait(act, a_c, t + 1)
                    wait(act, a_o, t - 1)
                    act.activation(QKT[p], ps[:, 3, :].rearrange("p (i n) -> p i n", i=4), ACT.Copy).then_inc(a_qkT, 1)

                def outputs(t):
                    wait(act, a_o, t + 1)
                    o = ps[:, 1, 0:NH * P].rearrange("p (h n) -> p h n", h=NH)
                    act.activation(OT[:, :, bass.ts(t, P)], o, ACT.Copy).then_inc(a_ow, 1)

                def step(t, p):
                    if not static(t, NT):
                        decays(t, p)
                    if not static(t, 0):
                        turned(t - 1, 1 - p)
                    if not static(t, 0) and not static(t, 1):
                        outputs(t - 2)
                    if not static(t, NT) and not static(t, NT - 1):
                        logs(t + 1, 1 - p)

                def turn(m):
                    for p in range(2):
                        step(2 * m + p, p)
                logs(0, 0)
                turns(act, turn, NT // 2 - 1)
                step(NT, 0)
                outputs(NT - 1)
                for h in range(2):
                    act.wait_ge(a_ow, NT // 2 * (h + 1))
                    act.activation(Os[h], OT[:, :, half(h)], ACT.Square).then_inc(f_sq, 1)
                for h in range(2):
                    act.wait_ge(f_ss, h + 1)
                    act.activation(Ol[h], ps[:, (6, 0)[h], :], ACT.Ln, bias=eps_rms[:, :]).then_inc(f_ln, 1)
                    act.wait_ge(f_ln, h + 1)
                    act.activation(Or[h], Ol[h], ACT.Exp, scale=-0.5).then_inc(f_r, 1)

            act.preload_act_table_set("natural_log_exp_and_others")
            act.wait_ge(s_set, 1)
            norm_scale(0)
            split_w1(0, 0, 0)
            router(0)
            ffn(0)
            act.preload_act_table_set("natural_log_exp_and_others")
            attention()
            norm_scale(2)
            split_w1(1, 0, 0)
            router(1)
            ffn(1)

        @block.gpsimd
        def _(pool):
            def ffn(f):
                def weigh(m, k):
                    u, p, h = TURN * m + k, k // 2 % 2, k % 2
                    wait(pool, s_hu, UNITS * f + u + 1)
                    if h == 0:
                        wait(pool, s_cb[p], 16 * (NJ // 2 * f + TURN // 4 * m + k // 4 + 1))
                    wait(pool, s_hl, UNITS * f + u - 1)
                    pool.tensor_tensor(Hf[h], Hu[k], CB[p][:, half(h)], ALU.mult).then_inc(s_tc, 1)

                def turn(m):
                    for k in range(TURN):
                        weigh(m, k)
                turn(0)
                with pool.Fori(1, NM) as m:
                    turn(m)

            def attention():
                for k in range(KD):
                    pool.wait_ge(a_wh, k + 1)
                    pool.tensor_tensor(WL[k][:, :], WA[:, k, :], WH[k][:, :].bitcast(F32), ALU.subtract).then_inc(a_wl, 1)

                def stage(t, p):
                    if static(t, 0):
                        pool.wait_ge(a_v, NT)
                    wait(pool, a_o, t - 1)
                    pool.tensor_copy(Va[p], VV[:, bass.ds(t, 1), :].rearrange("p a n -> p (a n)")).then_inc(a_va, 1)

                def k_rem(t, p):
                    wait(pool, a_k, t + 1)
                    wait(pool, a_e3, t + 1)
                    e3 = E13[p][:, D:2 * D]
                    pool.tensor_tensor(e3, Ka[p][:, :], e3, ALU.mult).then_inc(a_kr, 1)

                def turn(m):
                    for p in range(2):
                        stage(2 * m + p, p)
                        k_rem(2 * m + p, p)
                turn(0)
                with pool.Fori(1, NT // 2) as m:
                    turn(m)

            ffn(0)
            attention()
            ffn(1)

        @block.vector
        def _(dve):
            chain = [0]

            def link(ins):
                chain[0] += 1
                ins.then_inc(s_chain, 1)
                dve.wait_ge(s_chain, chain[0])

            def over_k(a):
                return spread(a, 1, KD)

            def norm(c):
                def centre(q):
                    dve.wait_ge(s_mean, NQ * c + q + 1)
                    dve.tensor_tensor(Dv[:, q, :, :], X[:, :, quarter(q)], over_k(ps[:, 4 + q, 0:QUART]),
                                      ALU.subtract).then_inc(s_d, 1)

                def scale(q):
                    dve.wait_ge(s_rs, NQ * c + q + 1)
                    dve.wait_ge(s_d, NQ * c + q + 1)
                    dve.tensor_tensor(XN[:, :, quarter(q)], Dv[:, q, :, :], over_k(Rs[q]), ALU.mult).then_inc(s_xn, 1)

                def low(q):
                    dve.wait_ge(s_xh, NQ * c + q + 1)
                    dve.tensor_tensor(XL[:, :, quarter(q)], XN[:, :, quarter(q)], XH[:, :, quarter(q)].bitcast(F32),
                                      ALU.subtract).then_inc(s_xl, 1)

                centre(0)
                centre(1)
                for q in range(2, NQ):
                    centre(q)
                    scale(q - 2)
                scale(NQ - 2)
                low(0)
                scale(NQ - 1)
                for q in range(1, NQ):
                    low(q)

            def split_w(f, j, p, cols, high, done):
                wait(dve, high, NJ * f + j + 1)
                w = WR[:, bass.ds(j, 1), cols].rearrange("p a n -> p (a n)")
                dve.tensor_tensor(WL[p][:, cols], w, WH[p][:, cols].bitcast(F32), ALU.subtract).then_inc(done, 1)

            def split_w1(f, j, p):
                split_w(f, j, p, W1, s_w1h, s_w1l)

            def split_w2(f, j, p):
                split_w(f, j, p, W2, s_w2h, s_w2l)

            def experts(a):
                return spread(a, 2, NE)

            def router(f):
                dve.wait_ge(s_lg, f + 1)
                logit = ps[:, 0, 0:NT * NC].rearrange("p (t c) -> p t c", c=NC)[:, :, 0:NE]
                link(dve.tensor_reduce(t1[:, :], logit, AX.X, ALU.max))
                dve.tensor_tensor(lg[:, :, :], logit, experts(t1[:, :]), ALU.subtract).then_inc(s_lgc, 1)
                dve.wait_ge(s_ex, f + 1)
                link(dve.tensor_reduce(t1[:, :], pe_[:, :, :], AX.X, ALU.add))
                link(dve.reciprocal(t2[:, :], t1[:, :]))
                link(dve.tensor_tensor(pr[:, :, :], pe_[:, :, :], experts(t2[:, :]), ALU.mult))
                for t in range(NT - 1):
                    dve.max(m8[:, t, :], pr[:, t, :])
                link(dve.max(m8[:, NT - 1, :], pr[:, NT - 1, :]))
                kth = experts(m8[:, :, TOPK - 1])
                dve.tensor_tensor(gt[:, :, :], pr[:, :, :], kth, ALU.is_gt)
                link(dve.tensor_tensor(eq[:, :, :], pr[:, :, :], kth, ALU.is_equal))
                dve.tensor_reduce(t1[:, :], gt[:, :, :], AX.X, ALU.add)
                link(dve.tensor_copy(cs[0][:, :, NE:2 * NE], eq[:, :, :]))
                a = 0
                for shift in (1, 2, 4, 8):
                    link(dve.tensor_tensor(cs[1 - a][:, :, NE:2 * NE], cs[a][:, :, NE:2 * NE],
                                           cs[a][:, :, NE - shift:2 * NE - shift], ALU.add))
                    a = 1 - a
                link(dve.tensor_tensor(lg[:, :, :], cs[a][:, :, NE:2 * NE], experts(t1[:, :]), ALU.add))
                link(dve.scalar_tensor_tensor(pe_[:, :, :], lg[:, :, :], float(TOPK), eq[:, :, :], ALU.is_le, ALU.mult))
                link(dve.tensor_tensor(gt[:, :, :], gt[:, :, :], pe_[:, :, :], ALU.add))
                dve.tensor_tensor(cf[:, :, 0:NE], pr[:, :, :], gt[:, :, :], ALU.mult)
                dve.wait_ge(s_sgx, f + 1)
                link(dve.tensor_scalar(t2[:, :], sgt[:, :], 1.0, None, ALU.add))
                dve.reciprocal(cf[:, :, NE], t2[:, :]).then_inc(s_coef, 1)

            def ffn(f):
                def hidden(m, k):
                    u, h = TURN * m + k, k % 2
                    wait(dve, s_si, UNITS * f + u + 1)
                    wait(dve, s_u, UNITS * f + u + 1)
                    wait(dve, s_tc, UNITS * f + u + 1 - TURN)
                    dve.tensor_tensor(Hu[k], ps[:, 6 + h, :], Sg[h], ALU.mult).then_inc(s_hu, 1)

                def low(u, h):
                    wait(dve, s_hh, UNITS * f + u + 1)
                    dve.tensor_tensor(HL[h][:, :], Hf[h], HH[h][:, :].bitcast(F32), ALU.subtract).then_inc(s_hl, 1)

                def turn(m):
                    for k in range(TURN):
                        hidden(m, k)
                        ffn_turn(f, m, k, low, split_w1, split_w2)
                turns(dve, turn, NM - 1)
                ffn_tail(f, low, split_w2)
                for q in range(NQ):
                    h = q // 2
                    dve.wait_ge(s_l2, UNITS * (f + 1) - 1 + h)
                    dve.scalar_tensor_tensor(X[:, :, quarter(q)], ps[:, 2 * h:2 * h + 2, q % 2 * QUART:(q % 2 + 1) * QUART], 0.5,
                                             X[:, :, quarter(q)], ALU.mult, ALU.add).then_inc(s_xr, 1)

            def attention():
                norm(1)
                for t in range(NT):
                    dve.wait_ge(a_sg, t + 1)
                    dve.tensor_tensor(GQ[:, t, D:2 * D], ps[:, t % 2, D:2 * D], GQ[:, t, D:2 * D], ALU.mult).then_inc(a_q, 1)
                for k in range(NH):
                    ins = dve.tensor_scalar(WO[:, k, :], WO[:, k, :], nw[:, k:k + 1], None, ALU.mult)
                ins.then_inc(a_wo, 1)

                def keys(t, p):
                    wait(dve, a_ex, t + 1)
                    dve.tensor_scalar(Ka[p][:, :], Ka[p][:, :], -1.0, 1.0, ALU.mult, ALU.add).then_inc(a_k, 1)

                def decayed(t, p):
                    if static(t, 0):
                        dve.wait_ge(a_q, NT)
                    wait(dve, a_k, t + 1)
                    wait(dve, a_e3, t + 1)
                    q = GQ[:, bass.ds(t, 1), D:2 * D].rearrange("p a n -> p (a n)")
                    dve.tensor_tensor(E13[p][:, 0:D], q, E13[p][:, 0:D], ALU.mult)
                    dve.tensor_tensor(E2[p], Ka[p][:, :], E2[p], ALU.mult).then_inc(a_qk, 1)

                def states(t, p):
                    wait(dve, a_st, t)
                    wait(dve, a_o, t - 1)
                    wait(dve, a_kv, t + 1)
                    for c in range(2):
                        if c == 1:
                            dve.copy_predicated(SM[p][:, :], tri2, ps[:, 2, 0:NH * P]).then_inc(a_sm, 1)
                            wait(dve, a_s1, t + 1)
                            wait(dve, a_o, t)
                        to = ST[(2 * p + c + 1) % 4]
                        for h in range(NH):
                            ins = dve.scalar_tensor_tensor(to[:, h, :], ST[2 * p + c][:, h, :], DC[p][:, h, c:c + 1],
                                                           kv_bank(h, c), ALU.mult, ALU.add)
                        ins.then_inc((a_s1, a_st)[c], 1)

                def step(t, p):
                    if not static(t, NT):
                        decayed(t, p)
                    if not static(t, 0):
                        states(t - 1, 1 - p)
                    if not static(t, NT) and not static(t, NT - 1):
                        keys(t + 1, 1 - p)

                def turn(m):
                    for p in range(2):
                        step(2 * m + p, p)
                keys(0, 0)
                turns(dve, turn, NT // 2 - 1)
                step(NT, 0)
                for h in range(2):
                    dve.wait_ge(f_y, h + 1)
                    dve.wait_ge(f_r, h + 1)
                    b = (4, 2)[h]
                    for q in (2 * h, 2 * h + 1):
                        c = slice(q % 2 * QUART, (q % 2 + 1) * QUART)
                        dve.tensor_tensor(Dv[:, q, :, :], ps[:, b:b + 2, c], over_k(Or[h][:, c]), ALU.mult).then_inc(f_t, 1)
                    for q in (2 * h, 2 * h + 1):
                        dve.wait_ge(f_t, q + 1)
                        dve.tensor_tensor(X[:, :, quarter(q)], X[:, :, quarter(q)], Dv[:, q, :, :], ALU.add).then_inc(s_xr, 1)

            dve.memset(mean_of[:, :], 1.0 / D)
            dve.memset(zeros[:, :], 0.0)
            dve.memset(eps_ln[:, :], LN_EPS)
            dve.memset(eps_rms[:, :], RMS_EPS)
            dve.memset(one[:, :], 1.0).then_inc(s_set, 1)
            for a in range(2):
                dve.memset(cs[a][:, :, 0:NE], 0.0)
                dve.memset(SM[a][:, :], 0.0)
            link(dve.memset(ST[0][:, :, :], 0.0))
            norm(0)
            split_w1(0, 0, 0)
            router(0)
            ffn(0)
            attention()
            norm(2)
            split_w1(1, 0, 0)
            router(1)
            ffn(1)


def layout(inputs):
    a = {k: np.asarray(v) for k, v in inputs.items()}

    def tiles(w):
        return np.ascontiguousarray(w.reshape(-1, P, w.shape[1]).transpose(1, 0, 2))

    w13, w2 = a["L0_ffn_w13"], a["L0_ffn_w2"]
    sgu, sd = a["L0_ffn_shared_gate_up_w"], a["L0_ffn_shared_down_w"]
    pad = np.zeros((NJ * P - NE * FE - FS, D), w13.dtype)
    gate = np.concatenate([w13[:, :FE].reshape(-1, D), sgu[:FS], pad])
    up = np.concatenate([w13[:, FE:].reshape(-1, D), sgu[FS:], pad])
    down = np.concatenate([w2.transpose(0, 2, 1).reshape(-1, D), sd.T, pad])
    w = np.empty((NJ, P, WC), w13.dtype)
    for i, m in enumerate((gate, up)):
        part = m.reshape(NJ, P, KD, P).transpose(0, 3, 2, 1)
        w[:, :, i * KD * P:(i + 1) * KD * P] = part.reshape(NJ, P, KD * P)
    w[:, :, 2 * KD * P:] = down.reshape(NJ, P, D)

    s, t = np.arange(P)[:, None], np.arange(P)[None, :]
    same = s // CH == t // CH
    tri = (same & (s <= t)).astype(np.float32)
    c = np.zeros((P, C_ALL), np.float32)
    c[:, C_ID:C_ID + P] = np.eye(P)
    c[:, C_TRI:C_TRI + P] = tri
    c[:, C_TRI + P:C_TRI + 2 * P] = tri
    c[:, C_REM:C_REM + P] = same & (s > t)
    c[:, C_CHUNK:C_CHUNK + 2] = s // CH == np.arange(2)[None, :]
    return {
        "xT": tiles(a["L0_attn_x"][0].T),
        "wffn": w,
        "wgate": tiles(np.concatenate([a["L0_ffn_gate_w"], a["L0_ffn_sgate_w"]]).T),
        "wkqv": tiles(np.concatenate([a["L0_attn_Wk"], a["L0_attn_Wq"], a["L0_attn_Wv"]]).T),
        "woT": tiles(a["L0_attn_Wo"].T),
        "normw": np.ascontiguousarray(a["L0_attn_norm_w"].reshape(NH, P).T),
        "consts": c,
    }


def kernel(**inputs):
    import concourse.bacc as bacc
    from concourse.bass_utils import run_bass_kernel_spmd

    nc = bacc.Bacc("TRN2", target_bir_lowering=False, num_devices=1)
    arrays = layout(inputs)
    args = [nc.dram_tensor(k, v.shape, mybir.dt.from_np(v.dtype), kind="ExternalInput").ap() for k, v in arrays.items()]
    out = nc.dram_tensor("out_t", (P, KD, N), F32, kind="ExternalOutput").ap()
    macaron(nc, *args, out)
    r = run_bass_kernel_spmd(nc, [arrays], core_ids=[0])
    y = r.results[0]["out_t"]
    return np.ascontiguousarray(y.transpose(2, 1, 0).reshape(1, N, D))
```

```python
from contextlib import ExitStack

import numpy as np

import concourse.bass as bass
from concourse import mybir

F32 = mybir.dt.float32
F32R = mybir.dt.float32r
I32 = mybir.dt.int32
ALU = mybir.AluOpType
ACT = mybir.ActivationFunctionType
AX = mybir.AxisListType

P = 128
N = 1024
D = 256
KD = D // P
HALF = 512
NE, TOPK = 16, 4
FE, FS = 176, 704
GRP = 16
NJ = -(-(NE * FE + FS) // P)
LAST = P // 2
assert NE * FE + FS == (NJ - 1) * P + LAST
NG = NJ * P // GRP
WC = 2 * KD * P + D
NC = NE + 1
NT = N // P
CH = 64
NH = 2
LN_EPS, RMS_EPS = 1e-5, 1e-6
UNITS = 2 * NJ
TURN = 8
NM = UNITS // TURN
LAG = 7
SPLIT = LAG - 1
RUN = 8
NQ, QUART = 4, N // 4

C_ID, C_TRI = 0, 128
C_ALL = 384


def spread(a, axis, n):
    a = a.unsqueeze(axis)
    shape = list(a.shape)
    shape[axis] = n
    return a.broadcast_to(shape)


def macaron(nc, xT, wffn, wgate, wkqv, woT, normw, consts, out):
    ctx = ExitStack()

    def sb(name, shape, dt=F32):
        return ctx.enter_context(nc.sbuf_tensor(name, shape, dt))

    def sem(name):
        return ctx.enter_context(nc.semaphore(name))

    with ctx:
        ps = ctx.enter_context(nc.psum_tensor("ps", [P, 8, HALF], F32))
        coef_dram = nc.dram_tensor("coef_groups", [NG, N], F32, kind="Internal").ap()
        cst = sb("cst", [P, C_ALL])
        X = sb("X", [P, KD, N])
        XN = sb("XN", [P, KD, N])
        XH = sb("XH", [P, KD, N], F32R)
        XL = sb("XL", [P, KD, N], F32R)
        WR = sb("WR", [P, NJ, WC])
        WH = [sb(f"WH{p}", [P, WC], F32R) for p in range(2)]
        WL = [sb(f"WL{p}", [P, WC], F32R) for p in range(2)]
        WG = sb("WG", [P, KD, NC])
        WA = sb("WA", [P, KD, 3 * D])
        WO = sb("WO", [P, NH, D])
        nw = sb("nw", [P, NH])
        eps_ln = sb("eps_ln", [P, 1])
        eps_rms = sb("eps_rms", [P, 1])
        one = sb("one", [P, 1])
        zeros = sb("zeros", [P, HALF], mybir.dt.bfloat16)
        mean_of = sb("mean_of", [P, P])
        ar = sb("ar", [P, 15 * HALF])

        def area(at, n):
            return ar[:, at:at + n]

        Dv = sb("Dv", [P, NQ, KD, QUART])
        Sq = [area(q * HALF, HALF).rearrange("p (k n) -> p k n", k=KD) for q in range(NQ)]
        Lv = [area(4 * HALF + q * QUART, QUART) for q in range(NQ)]
        Rs = [area(6 * HALF + q * QUART, QUART) for q in range(NQ)]
        STAT_BANK = (4, 6, 5, 7)
        CB = [area(2 * p * HALF, N) for p in range(2)]
        Sg = [area((4 + h) * HALF, HALF) for h in range(2)]
        Hu = [area((6 + i) * HALF, HALF) for i in range(TURN)]
        Hf = [Dv[:, h, :, :].rearrange("p k n -> p (k n)") for h in range(2)]
        HH = [sb(f"HH{h}", [P, HALF], F32R) for h in range(2)]
        HL = [sb(f"HL{h}", [P, HALF], F32R) for h in range(2)]
        lg = sb("lg", [P, NT, NE])
        pe_ = sb("pe_", [P, NT, NE])
        pr = sb("pr", [P, NT, NE])
        m8 = sb("m8", [P, NT, 8])
        t1 = sb("t1", [P, NT])
        t2 = sb("t2", [P, NT])
        sgt = sb("sgt", [P, NT])
        gt = sb("gt", [P, NT, NE])
        eq = sb("eq", [P, NT, NE])
        cs = [sb(f"cs{i}", [P, NT, 2 * NE]) for i in range(2)]
        cf = sb("cf", [P, NT, NC])
        scratch = sb("scratch", [P, N])
        cT = scratch[0:NC, :]
        A = area(0, 2 * N).rearrange("p (h n) -> p h n", h=NH)
        K = area(2 * N, 2 * N).rearrange("p (h n) -> p h n", h=NH)
        Q = area(4 * N, 2 * N).rearrange("p (h n) -> p h n", h=NH)
        E1 = XN
        V = Dv.rearrange("p q k n -> p (q k) n")
        ones = scratch[:, 0:QUART]
        Kg = [area(12 * HALF + p * D, D).rearrange("p (h n) -> p h n", h=NH) for p in range(2)]
        Qd = [area(13 * HALF + p * D, D).rearrange("p (h n) -> p h n", h=NH) for p in range(2)]
        Kt = [area(14 * HALF + p * D, D) for p in range(2)]
        Va = [sb(f"Va{p}", [P, D]) for p in range(2)]
        Su = sb("Su", [P, NH, P])
        DC = [sb(f"DC{p}", [P, NH, 2]) for p in range(2)]
        SM = [sb(f"SM{p}", [P, NH * P]) for p in range(2)]
        ST = [sb(f"ST{i}", [P, NH, P]) for i in range(4)]
        OT = XN
        Os = [a.rearrange("p (k n) -> p k n", k=NH) for a in
              (scratch[:, HALF:2 * HALF], scratch[:, 0:HALF], area(0, HALF), area(HALF, HALF))]
        Ol = [area(10 * HALF + q * QUART, QUART) for q in range(NQ)]
        Or = [area(2 * HALF + q * QUART, QUART) for q in range(NQ)]
        Yr = [area(at * HALF, HALF).rearrange("p (k n) -> p k n", k=KD) for at in (4, 5, 8, 9)]
        SS_BANK, Y_BANK = (6, 7, 0, 1), (4, 5, 3, 2)

        ident = cst[:, C_ID:C_ID + P]
        tri2 = cst[:, C_TRI:C_TRI + NH * P].bitcast(I32)

        s_xin = [sem(f"s_xin{q}") for q in range(NQ)]
        s_cst, s_wg, s_wa, s_out, s_cg = (sem(n) for n in ("s_cst", "s_wg", "s_wa", "s_out", "s_cg"))
        s_wr = [sem(f"s_wr{p}") for p in range(2)]
        s_cb = [sem(f"s_cb{p}") for p in range(2)]
        s_set = sem("s_set")
        s_mean, s_d, s_sq, s_var, s_ln, s_rs, s_xn, s_xh, s_xl, s_xr = (
            sem(n) for n in "s_mean s_d s_sq s_var s_ln s_rs s_xn s_xh s_xl s_xr".split())
        s_lg, s_lgc, s_ex, s_sgx, s_coef, s_ct, s_cts, s_chain = (
            sem(n) for n in "s_lg s_lgc s_ex s_sgx s_coef s_ct s_cts s_chain".split())
        s_w1h, s_w1l, s_w2h, s_w2l, s_g, s_u, s_si, s_hu, s_tc, s_hh, s_hl, s_l2 = (
            sem(n) for n in "s_w1h s_w1l s_w2h s_w2l s_g s_u s_si s_hu s_tc s_hh s_hl s_l2".split())
        a_wh, a_wl, a_kp, a_qp, a_sk, a_sq, a_q, a_wo = (sem("a_" + n) for n in "wh wl kp qp sk sq q wo".split())
        a_ones, a_g, a_L, a_f, a_A, a_e = (sem("a_" + n) for n in "ones g L f A e".split())
        a_vp, a_v, a_va, a_kg, a_qk, a_c, a_kt, a_dc, a_sc, a_kv, a_sm, a_su, a_s1, a_st, a_o, a_ow = (
            sem("a_" + n) for n in "vp v va kg qk c kt dc sc kv sm su s1 st o ow".split())
        f_sq, f_ss, f_ln, f_r, f_y, f_t = (sem("f_" + n) for n in "sq ss ln r y t".split())

        block = ctx.enter_context(nc.Block())

        def wait(eng, s, v):
            if isinstance(v, int) and v <= 0:
                return
            eng.wait_ge(s, v)

        def half(h):
            return slice(h * HALF, (h + 1) * HALF)

        def quarter(q):
            return slice(q * QUART, (q + 1) * QUART)

        def static(x, value=None):
            return isinstance(x, int) and value in (None, x)

        W2 = slice(2 * KD * P, WC)

        def w1(j):
            return slice(0, KD * P) if static(j, NJ - 1) else slice(0, 2 * KD * P)

        def is_last(u):
            return static(u) and u >= UNITS - 2

        def rows(u):
            return slice(P - LAST, P) if is_last(u) else slice(0, P)

        def split_buffers(u, h):
            if static(u) and u >= UNITS - 4:
                return [a[:, u % 2, half(u // 2 % 2)] for a in (XH, XL)]
            return [a[h][:, :] for a in (HH, HL)]

        def kv_bank(c):
            return ps[:, 6 + c, 0:NH * P].rearrange("p (h n) -> p h n", h=NH)

        def turns(eng, body, last):
            body(0)
            with eng.Fori(1, last) as m:
                body(m)
            body(last)

        def ffn_turn(f, m, k, split_h, split_w1, split_w2):
            if k % 2 == 0 and not (static(m, NM - 1) and k == TURN - 2) and not (static(m, 0) and k == 0):
                split_w1(f, TURN // 2 * m + k // 2 + 1, (k // 2 + 1) % 2)
            if not static(m, 0) or k >= SPLIT:
                split_h(TURN * m + k - SPLIT, k % 2)
            if k % 2 == 1 and (not static(m, 0) or k >= SPLIT - 1):
                j = (k - SPLIT + 1) // 2
                split_w2(f, TURN // 2 * m + j, j % 2)

        def ffn_tail(f, split_h, split_w2):
            for k in range(SPLIT):
                split_h(UNITS + k - SPLIT, k % 2)
                if k % 2 == 1 and k < SPLIT - 1:
                    j = NJ + (k - SPLIT + 1) // 2
                    split_w2(f, j, j % 2)

        @block.sync
        def _(sp):
            def load_w(j, p):
                sp.dma_start(WR[:, bass.ds(j, 1), :], wffn[bass.ds(j, 1), :, :].rearrange("a p n -> p a n")).then_inc(s_wr[p], 16)

            def load_cb(j, p):
                src = coef_dram[bass.ds(j * (P // GRP), P // GRP), :]
                sp.dma_start(CB[p], spread(src, 1, GRP)).then_inc(s_cb[p], 16)

            for q in range(NQ):
                sp.dma_start(X[:, :, quarter(q)], xT[:, :, quarter(q)]).then_inc(s_xin[q], 16)
            sp.dma_start(WG[:, :, :], wgate).then_inc(s_wg, 16)
            for j in range(RUN):
                if j >= 2:
                    sp.wait_ge(s_wr[j % 2], 16 * (j // 2))
                load_w(j, j % 2)
                if j == 1:
                    sp.dma_start(cst[:, :], consts).then_inc(s_cst, 16)
            sp.dma_start(WA[:, :, :], wkqv).then_inc(s_wa, 16)
            sp.dma_start(WO[:, :, :], woT).then_inc(s_wa, 16)
            sp.dma_start(nw[:, :], normw).then_inc(s_wa, 16)

            for f in range(2):
                sp.wait_ge(s_cts, f + 1)
                er = NE * (FE // GRP)
                rows = coef_dram[0:er, :].rearrange("(e r) n -> e r n", r=FE // GRP)
                sp.dma_start(rows, spread(cT[0:NE, :], 1, FE // GRP)).then_inc(s_cg, 16)
                sp.dma_start(coef_dram[er:NG, :].rearrange("(a r) n -> a r n", a=1),
                             spread(cT[NE:NC, :], 1, NG - er)).then_inc(s_cg, 16)
                sp.wait_ge(s_cg, 32 * (f + 1))
                for p in range(2):
                    load_cb(p, p)

                def turn(m, weights, slices=TURN // 2):
                    for k in range(slices):
                        p = k % 2
                        if weights:
                            sp.wait_ge(s_wr[p], 16 * (m * (TURN // 4) + (k + RUN) // 2))
                            load_w(m * (TURN // 2) + k + RUN, p)
                        sp.wait_ge(s_tc, UNITS * f + TURN * m + 2 * k + 2)
                        load_cb(m * (TURN // 2) + k + 2, p)

                if f == 0:
                    with sp.Fori(0, NM - 2) as m:
                        turn(m, True)
                    turn(NM - 2, False)
                else:
                    with sp.Fori(0, NM - 1) as m:
                        turn(m, False)
                turn(NM - 1, False, TURN // 2 - 2)

            for q in range(NQ):
                sp.wait_ge(s_xr, 2 * NQ + q + 1)
                sp.dma_start(out[:, :, quarter(q)], X[:, :, quarter(q)]).then_inc(s_out, 16)
            sp.wait_ge(s_out, 16 * NQ)

        @block.tensor
        def _(pe):
            def keep_warm(n, bank):
                for _ in range(n):
                    pe.matmul(ps[:, bank, :], zeros[:, 0:P], zeros[:, :], start=True, stop=True)

            def stat(q, of_squares):
                for k in range(KD):
                    x = Sq[q][:, k, :] if of_squares else X[:, k, quarter(q)]
                    mm = pe.matmul(ps[:, STAT_BANK[q], 0:QUART], mean_of[:, :], x, start=k == 0, stop=k == KD - 1)
                mm.then_inc(s_var if of_squares else s_mean, 1)

            def mean(c, q):
                if c == 0:
                    pe.wait_ge(s_xin[q], 16)
                else:
                    pe.wait_ge(s_xr, NQ * (c - 1) + q + 1)
                stat(q, False)

            def var(c, q):
                pe.wait_ge(s_sq, NQ * c + q + 1)
                stat(q, True)

            def norm_stats(c, begun=0):
                if c == 0:
                    pe.wait_ge(s_set, 1)
                    keep_warm(6, 3)
                for q in range(begun, 2):
                    mean(c, q)
                for q in range(2, NQ):
                    var(c, q - 2)
                    mean(c, q)
                for q in range(2, NQ):
                    var(c, q)

            def logit(f, t):
                if t == 0 and f == 0:
                    pe.wait_ge(s_wg, 16)
                pe.wait_ge(s_xn, 2 * NQ * f + t * P // QUART + 1)
                for k in range(KD):
                    mm = pe.matmul(ps[:, 0, t * NC:(t + 1) * NC], XN[:, k, t * P:(t + 1) * P], WG[:, k, :],
                                   start=k == 0, stop=k == KD - 1)
                if t == NT - 1:
                    mm.then_inc(s_lg, 1)

            def turn_coefs(f):
                if f == 0:
                    pe.wait_ge(s_cst, 16)
                pe.wait_ge(s_coef, f + 1)
                for t in range(NT):
                    mm = pe.transpose(ps[0:NC, 1 + t // 4, (t % 4) * P:(t % 4 + 1) * P], cf[:, t, :], ident)
                mm.then_inc(s_ct, 1)

            def clear(f):
                pe.wait_ge(s_cts, f + 1)
                for bank in range(4):
                    pe.matmul(ps[:, bank, :], zeros[:, 0:P], zeros[:, :], start=True, stop=False, skip_group_check=True)

            def first(f, u, j, p, h):
                if static(u) and u < 2:
                    pe.wait_ge(s_xl, 2 * f * NQ + 2 * h + 2)
                if h == 0:
                    wait(pe, s_w1l, NJ * f + j + 1)
                layers = ((0, 4, s_g, s_si), (1, 6, s_u, s_hu))
                for what, bank, done, freed in layers[:1] if is_last(u) else layers:
                    wait(pe, freed, UNITS * f + u - 1)
                    n = 0
                    for w, x in ((WH, XH), (WH, XL), (WL, XH)):
                        for k in range(KD):
                            col = (what * KD + k) * P
                            mm = pe.matmul(ps[:, bank + h, :], w[p][:, col:col + P], x[:, k, half(h)],
                                           start=n == 0, stop=n == 5)
                            if n == 5:
                                mm.then_inc(done, 1)
                            n += 1
                            if static(u, 0) and 6 * what + n <= NT:
                                logit(f, 6 * what + n - 1)

            def second(f, u, j, p, h, stop):
                if h == 0:
                    wait(pe, s_w2l, NJ * f + j + 1)
                wait(pe, s_hl, UNITS * f + u + 1)
                hh, hl = split_buffers(u, h)
                if is_last(u):
                    passes = ((WH, hh, slice(0, P)), (WL, hh, rows(u)))
                else:
                    passes = ((WH, hh, slice(0, P)), (WH, hl, slice(0, P)), (WL, hh, slice(0, P)))
                for n, (w, x, r) in enumerate(passes):
                    for k in range(KD):
                        col = 2 * KD * P + k * P
                        mm = pe.matmul(ps[:, 2 * h + k, :], w[p][r, col:col + P], x[r, :], start=False,
                                       stop=stop and n == len(passes) - 1, skip_group_check=True)
                mm.then_inc(s_l2, 1)

            def ffn(f):
                def late(m, k):
                    second(f, TURN * m + k, TURN // 2 * m + k // 2, k // 2 % 2, k % 2,
                           static(m, NM - 1) and k >= TURN - 2)

                def turn(m):
                    for k in range(TURN):
                        first(f, TURN * m + k, TURN // 2 * m + k // 2, k // 2 % 2, k % 2)
                        if static(m, 0) and k == 2:
                            turn_coefs(f)
                        if static(m, 0) and k == LAG:
                            clear(f)
                        if not static(m, 0) or k >= LAG:
                            late(m, k - LAG)
                turns(pe, turn, NM - 1)
                for k in range(TURN - LAG, TURN):
                    late(NM - 1, k)

            def attention():
                pe.wait_ge(a_wl, KD)

                def project(h, e, cols, bank, done):
                    n = 0
                    for w, x in ((WH, XH), (WH, XL), (WL, XH)):
                        for k in range(KD):
                            mm = pe.matmul(ps[:, bank + 2 * h + e, :], w[k][:, cols + e * P:cols + (e + 1) * P], x[:, k, half(h)],
                                           start=n == 0, stop=n == 5)
                            n += 1
                    mm.then_inc(done, 1)

                for cols, bank, done in ((0, 0, a_kp), (D, 4, a_qp)):
                    for h in range(2):
                        pe.wait_ge(s_xl, NQ + 2 * h + 2)
                        for e in range(NH):
                            project(h, e, cols, bank, done)
                for t in range(NT):
                    pe.wait_ge(a_sk, t // 2 + 1)
                    n = 0
                    for x, w in ((XH, WH), (XL, WH), (XH, WL)):
                        for k in range(KD):
                            mm = pe.matmul(ps[:, t // 2, t % 2 * D:(t % 2 + 1) * D], x[:, k, t * P:(t + 1) * P], w[k][:, 2 * D:3 * D],
                                           start=n == 0, stop=n == 5)
                            n += 1
                    if t % 2 == 1:
                        mm.then_inc(a_vp, 1)
                pe.wait_ge(a_q, 4)
                keep_warm(6, 4)
                pe.wait_ge(a_v, NT // 2)

                def turn_k(t, p):
                    wait(pe, a_kg, t + 1)
                    wait(pe, a_kt, t)
                    for h in range(NH):
                        mm = pe.transpose(ps[:, 3, h * P:(h + 1) * P], Kg[p][:, h, :], ident)
                    mm.then_inc(a_c, 1)

                def scores(t, p):
                    wait(pe, a_qk, t + 1)
                    wait(pe, a_sm, t)
                    for h in range(NH):
                        mm = pe.matmul(ps[:, 2, h * P:(h + 1) * P], Kg[p][:, h, :], Qd[p][:, h, :], start=True, stop=True)
                    mm.then_inc(a_sc, 1)

                def kv(t, p):
                    wait(pe, a_kt, t + 1)
                    wait(pe, a_va, t + 1)
                    wait(pe, a_st, t)
                    for h in range(NH):
                        for c in range(2):
                            r = slice(c * CH, (c + 1) * CH)
                            mm = pe.matmul(kv_bank(c)[:, h, :], Kt[p][r, h * P:(h + 1) * P],
                                           Va[p][r, h * P:(h + 1) * P], start=True, stop=True)
                    mm.then_inc(a_kv, 1)

                def outputs(t, p):
                    wait(pe, a_sm, t + 1)
                    wait(pe, a_ow, t)
                    for h in range(NH):
                        pe.matmul(ps[:, h, 0:P], Va[p][:, h * P:(h + 1) * P], SM[p][:, h * P:(h + 1) * P],
                                  start=True, stop=False, skip_group_check=True)
                    for c in range(2):
                        if c == 1:
                            wait(pe, a_s1, t + 1)
                        for h in range(NH):
                            mm = pe.matmul(ps[:, h, c * CH:(c + 1) * CH], ST[2 * p + c][:, h, :],
                                           Qd[p][:, h, c * CH:(c + 1) * CH], start=False, stop=c == 1, skip_group_check=True)
                    mm.then_inc(a_o, 1)

                def step(t, p):
                    if not static(t, 0):
                        kv(t - 1, 1 - p)
                    turn_k(t, p)
                    scores(t, p)
                    if not static(t, 0):
                        outputs(t - 1, 1 - p)

                def turn(m):
                    for p in range(2):
                        step(2 * m + p, p)

                def product(q):
                    if q == 0:
                        pe.wait_ge(a_wo, 1)
                    if q == 2:
                        pe.wait_ge(a_kt, NT)
                    if q == 3:
                        pe.wait_ge(a_st, NT)
                    pe.wait_ge(a_ow, NT // NQ * (q + 1))
                    for d in range(KD):
                        for k in range(NH):
                            mm = pe.matmul(ps[:, Y_BANK[q], d * QUART:(d + 1) * QUART], WO[:, k, d * P:(d + 1) * P],
                                           OT[:, k, quarter(q)], start=k == 0, stop=k == NH - 1)
                    mm.then_inc(f_y, 1)

                def rms(q):
                    pe.wait_ge(f_sq, q + 1)
                    if q == 0:
                        pe.wait_ge(a_st, NT)
                    if q == 2:
                        pe.wait_ge(a_ow, NT)
                    for k in range(NH):
                        mm = pe.matmul(ps[:, SS_BANK[q], 0:QUART], mean_of[:, :], Os[q][:, k, :], start=k == 0, stop=k == NH - 1)
                    mm.then_inc(f_ss, 1)

                step(0, 0)
                step(1, 1)
                with pe.Fori(1, NT // 2) as m:
                    turn(m)
                kv(NT - 1, 1)
                product(0)
                outputs(NT - 1, 1)
                product(1)
                rms(0)
                rms(1)
                product(2)
                rms(2)
                mean(2, 0)
                product(3)
                mean(2, 1)
                rms(3)

            for f in range(2):
                norm_stats(2 * f, 2 * f)
                ffn(f)
                if f == 0:
                    norm_stats(1)
                    attention()

        @block.scalar
        def _(act):
            def norm_scale(c):
                def square(q):
                    act.wait_ge(s_d, NQ * c + q + 1)
                    act.activation(Sq[q], Dv[:, q, :, :], ACT.Square).then_inc(s_sq, 1)

                def scale(q):
                    act.wait_ge(s_var, NQ * c + q + 1)
                    act.activation(Lv[q], ps[:, STAT_BANK[q], 0:QUART], ACT.Ln, bias=eps_ln[:, :]).then_inc(s_ln, 1)
                    act.wait_ge(s_ln, NQ * c + q + 1)
                    act.activation(Rs[q], Lv[q], ACT.Exp, scale=-0.5).then_inc(s_rs, 1)

                def high(q):
                    act.wait_ge(s_xn, NQ * c + q + 1)
                    act.activation(XH[:, :, quarter(q)], XN[:, :, quarter(q)], ACT.Copy).then_inc(s_xh, 1)

                for q in range(2):
                    square(q)
                for q in range(2):
                    scale(q)
                for q in range(2):
                    high(q)
                    square(q + 2)
                if c == 0:
                    split_w1(0, 0, 0)
                for q in range(2, NQ):
                    scale(q)
                for q in range(2, NQ):
                    high(q)

            def split_w(f, j, p, cols, freed, count, done):
                if f == 0:
                    act.wait_ge(s_wr[p], 16 * (j // 2 + 1) if static(j) else 8 * (j - p) + 16)
                wait(act, freed, count)
                w = WR[:, bass.ds(j, 1), cols].rearrange("p a n -> p (a n)")
                act.activation(WH[p][:, cols], w, ACT.Copy).then_inc(done, 1)

            def split_w1(f, j, p):
                split_w(f, j, p, w1(j), s_u, (UNITS - 2) * f + 2 * j - 2, s_w1h)

            def split_w2(f, j, p):
                split_w(f, j, p, W2, s_l2, UNITS * f + 2 * j - 2, s_w2h)

            def router(f):
                split_w1(f, 1, 1)
                act.wait_ge(s_lgc, f + 1)
                act.activation(pe_[:, :, :], lg[:, :, :], ACT.Exp).then_inc(s_ex, 1)
                sgate = ps[:, 0, 0:NT * NC].rearrange("p (t c) -> p t c", c=NC)[:, :, NE]
                act.activation(sgt[:, :], sgate, ACT.Exp, scale=-1.0).then_inc(s_sgx, 1)

            def ffn(f):
                def silu(u, h):
                    wait(act, s_g, UNITS * f + u + 1)
                    wait(act, s_hu, UNITS * f + u - 1)
                    gate = slice(0, LAST) if is_last(u) else rows(u)
                    act.activation(Sg[h][rows(u), :], ps[gate, 4 + h, :], ACT.Silu).then_inc(s_si, 1)

                def high(u, h):
                    wait(act, s_tc, UNITS * f + u + 1)
                    if static(u) and u >= UNITS - 4:
                        wait(act, s_g, UNITS * (f + 1))
                    else:
                        wait(act, s_l2, UNITS * f + u - 1)
                    act.activation(split_buffers(u, h)[0][rows(u), :], Hf[h][rows(u), :], ACT.Copy).then_inc(s_hh, 1)

                def turn(m):
                    for k in range(TURN):
                        if static(m, NM - 1):
                            ffn_turn(f, m, k, high, split_w1, split_w2)
                        silu(TURN * m + k, k % 2)
                        if static(m, 0) and k == 2:
                            act.wait_ge(s_ct, f + 1)
                            act.activation(cT, ps[0:NC, 1:3, :], ACT.Copy).then_inc(s_cts, 1)
                        if not static(m, NM - 1):
                            ffn_turn(f, m, k, high, split_w1, split_w2)
                turns(act, turn, NM - 1)
                ffn_tail(f, high, split_w2)

            def attention():
                for k in range(KD):
                    if k == 0:
                        act.wait_ge(s_l2, UNITS)
                        act.wait_ge(s_wa, 48)
                    act.activation(WH[k][:, :], WA[:, k, :], ACT.Copy).then_inc(a_wh, 1)
                norm_scale(1)
                act.preload_act_table(ACT.Sigmoid)
                for to, bank, done, out_done in ((A, 0, a_kp, a_sk), (Q, 4, a_qp, a_sq)):
                    for h in range(2):
                        for e in range(NH):
                            act.wait_ge(done, 2 * h + e + 1)
                            act.activation(to[:, e, half(h)], ps[:, bank + 2 * h + e, :], ACT.Sigmoid).then_inc(out_done, 1)
                act.preload_act_table_set("natural_log_exp_and_others")

                def logs(q):
                    g = A[:, :, quarter(q)]
                    act.wait_ge(a_sk, 4)
                    act.activation(g, g, ACT.Exp, scale=-1.0).then_inc(a_g, 1)
                    act.wait_ge(a_g, q + 1)
                    act.activation(g, g, ACT.Ln, bias=one[:, :]).then_inc(a_L, 1)
                    act.wait_ge(a_L, q + 1)
                    act.activation(K[:, :, quarter(q)], g, ACT.Exp, scale=-1.0).then_inc(a_f, 1)

                def decays(q):
                    act.wait_ge(a_A, q + 1)
                    a = A[:, :, quarter(q)]
                    act.activation(E1[:, :, quarter(q)], a, ACT.Exp, scale=-1.0)
                    act.activation(a, a, ACT.Exp).then_inc(a_e, 1)

                def turned(t, p):
                    wait(act, a_c, t + 1)
                    wait(act, a_kv, t - 1)
                    act.activation(Kt[p], ps[:, 3, 0:D], ACT.Copy).then_inc(a_kt, 1)

                def chunk_decays(t, p):
                    wait(act, a_st, t - 1)
                    ends = E1[:, :, bass.ts(t, P)].rearrange("p h (c n) -> p h c n", n=CH)[:, :, :, CH - 1]
                    act.activation(DC[p][:, :, :], ends, ACT.Copy).then_inc(a_dc, 1)

                def outputs(t):
                    wait(act, a_o, t + 1)
                    act.activation(OT[:, :, bass.ts(t, P)], ps[:, 0:NH, 0:P], ACT.Copy).then_inc(a_ow, 1)

                def step(t, p):
                    turned(t, p)
                    chunk_decays(t, p)
                    if not static(t, 0):
                        outputs(t - 1)

                def turn(m):
                    for p in range(2):
                        step(2 * m + p, p)

                def square(q):
                    act.wait_ge(a_ow, NT // NQ * (q + 1))
                    act.activation(Os[q], OT[:, :, quarter(q)], ACT.Square).then_inc(f_sq, 1)

                def rms(q):
                    act.wait_ge(f_ss, q + 1)
                    act.activation(Ol[q], ps[:, SS_BANK[q], 0:QUART], ACT.Ln, bias=eps_rms[:, :]).then_inc(f_ln, 1)
                    act.wait_ge(f_ln, q + 1)
                    act.activation(Or[q], Ol[q], ACT.Exp, scale=-0.5).then_inc(f_r, 1)

                logs(0)
                logs(1)
                decays(0)
                step(0, 0)
                logs(2)
                decays(1)
                step(1, 1)
                logs(3)
                decays(2)
                decays(3)
                with act.Fori(1, NT // 2) as m:
                    turn(m)
                split_w1(1, 0, 0)
                square(0)
                square(1)
                act.wait_ge(a_qk, NT)
                square(2)
                outputs(NT - 1)
                square(3)
                rms(0)
                for q in range(1, NQ):
                    rms(q)

            act.preload_act_table_set("natural_log_exp_and_others")
            act.wait_ge(s_set, 1)
            norm_scale(0)
            router(0)
            ffn(0)
            act.preload_act_table_set("natural_log_exp_and_others")
            attention()
            norm_scale(2)
            router(1)
            ffn(1)

        @block.gpsimd
        def _(pool):
            def ffn(f):
                def weigh(m, k):
                    u, p, h = TURN * m + k, k // 2 % 2, k % 2
                    wait(pool, s_hu, UNITS * f + u + 1)
                    if h == 0:
                        wait(pool, s_cb[p], 16 * (NJ // 2 * f + TURN // 4 * m + k // 4 + 1))
                    wait(pool, s_hl, UNITS * f + u - 1)
                    pool.tensor_tensor(Hf[h], Hu[k], CB[p][:, half(h)], ALU.mult).then_inc(s_tc, 1)

                def turn(m):
                    for k in range(TURN):
                        weigh(m, k)
                turn(0)
                with pool.Fori(1, NM) as m:
                    turn(m)

            def attention():
                for k in range(KD):
                    pool.wait_ge(a_wh, k + 1)
                    pool.tensor_tensor(WL[k][:, :], WA[:, k, :], WH[k][:, :].bitcast(F32), ALU.subtract).then_inc(a_wl, 1)

                pool.memset(ones, 1.0).then_inc(a_ones, 1)
                pool.wait_ge(a_ones, 1)
                pool.memset(ones.rearrange("p (c n) -> p c n", n=CH)[:, :, 0], 0.0).then_inc(a_ones, 1)

                def stage(t, p):
                    if static(t, 0):
                        pool.wait_ge(a_v, NT // 2)
                    wait(pool, a_o, t - 1)
                    pool.tensor_copy(Va[p][:, :], V[:, bass.ds(t, 1), :].rearrange("p a n -> p (a n)")).then_inc(a_va, 1)

                def turn(m):
                    for p in range(2):
                        stage(2 * m + p, p)
                turn(0)
                with pool.Fori(1, NT // 2) as m:
                    turn(m)

            ffn(0)
            attention()
            ffn(1)

        @block.vector
        def _(dve):
            chain = [0]

            def link(ins):
                chain[0] += 1
                ins.then_inc(s_chain, 1)
                dve.wait_ge(s_chain, chain[0])

            def over_k(a):
                return spread(a, 1, KD)

            def centre(c, q):
                dve.wait_ge(s_mean, NQ * c + q + 1)
                dve.tensor_tensor(Dv[:, q, :, :], X[:, :, quarter(q)], over_k(ps[:, STAT_BANK[q], 0:QUART]),
                                  ALU.subtract).then_inc(s_d, 1)

            def norm(c, begun=0):
                def scale(q):
                    dve.wait_ge(s_rs, NQ * c + q + 1)
                    dve.wait_ge(s_d, NQ * c + q + 1)
                    dve.tensor_tensor(XN[:, :, quarter(q)], Dv[:, q, :, :], over_k(Rs[q]), ALU.mult).then_inc(s_xn, 1)

                def low(q):
                    dve.wait_ge(s_xh, NQ * c + q + 1)
                    dve.tensor_tensor(XL[:, :, quarter(q)], XN[:, :, quarter(q)], XH[:, :, quarter(q)].bitcast(F32),
                                      ALU.subtract).then_inc(s_xl, 1)

                for q in range(begun, 2):
                    centre(c, q)
                scale(0)
                centre(c, 2)
                scale(1)
                centre(c, 3)
                low(0)
                low(1)
                if c == 0:
                    split_w1(0, 0, 0)
                scale(2)
                scale(3)
                low(2)
                low(3)

            def split_w(f, j, p, cols, high, done):
                wait(dve, high, NJ * f + j + 1)
                w = WR[:, bass.ds(j, 1), cols].rearrange("p a n -> p (a n)")
                dve.tensor_tensor(WL[p][:, cols], w, WH[p][:, cols].bitcast(F32), ALU.subtract).then_inc(done, 1)

            def split_w1(f, j, p):
                split_w(f, j, p, w1(j), s_w1h, s_w1l)

            def split_w2(f, j, p):
                split_w(f, j, p, W2, s_w2h, s_w2l)

            def experts(a):
                return spread(a, 2, NE)

            def hidden(f, m, k):
                u, h = TURN * m + k, k % 2
                wait(dve, s_si, UNITS * f + u + 1)
                if not is_last(u):
                    wait(dve, s_u, (UNITS - 2) * f + u + 1)
                wait(dve, s_tc, UNITS * f + u + 1 - TURN)
                up = (4 if is_last(u) else 6) + h
                dve.tensor_tensor(Hu[k][rows(u), :], ps[rows(u), up, :], Sg[h][rows(u), :], ALU.mult).then_inc(s_hu, 1)

            def router(f):
                split_w1(f, 1, 1)
                dve.wait_ge(s_lg, f + 1)
                logit = ps[:, 0, 0:NT * NC].rearrange("p (t c) -> p t c", c=NC)[:, :, 0:NE]
                link(dve.tensor_reduce(t1[:, :], logit, AX.X, ALU.max))
                dve.tensor_tensor(lg[:, :, :], logit, experts(t1[:, :]), ALU.subtract).then_inc(s_lgc, 1)
                dve.wait_ge(s_ex, f + 1)
                link(dve.tensor_reduce(t1[:, :], pe_[:, :, :], AX.X, ALU.add))
                link(dve.reciprocal(t2[:, :], t1[:, :]))
                link(dve.tensor_tensor(pr[:, :, :], pe_[:, :, :], experts(t2[:, :]), ALU.mult))
                for t in range(NT - 1):
                    dve.max(m8[:, t, :], pr[:, t, :])
                link(dve.max(m8[:, NT - 1, :], pr[:, NT - 1, :]))
                kth = experts(m8[:, :, TOPK - 1])
                dve.tensor_tensor(gt[:, :, :], pr[:, :, :], kth, ALU.is_gt)
                link(dve.tensor_tensor(eq[:, :, :], pr[:, :, :], kth, ALU.is_equal))
                dve.tensor_reduce(t1[:, :], gt[:, :, :], AX.X, ALU.add)
                link(dve.tensor_copy(cs[0][:, :, NE:2 * NE], eq[:, :, :]))
                a = 0
                for shift in (1, 2, 4, 8):
                    link(dve.tensor_tensor(cs[1 - a][:, :, NE:2 * NE], cs[a][:, :, NE:2 * NE],
                                           cs[a][:, :, NE - shift:2 * NE - shift], ALU.add))
                    a = 1 - a
                hidden(f, 0, 0)
                link(dve.tensor_tensor(lg[:, :, :], cs[a][:, :, NE:2 * NE], experts(t1[:, :]), ALU.add))
                link(dve.scalar_tensor_tensor(pe_[:, :, :], lg[:, :, :], float(TOPK), eq[:, :, :], ALU.is_le, ALU.mult))
                link(dve.tensor_tensor(gt[:, :, :], gt[:, :, :], pe_[:, :, :], ALU.add))
                dve.tensor_tensor(cf[:, :, 0:NE], pr[:, :, :], gt[:, :, :], ALU.mult)
                dve.wait_ge(s_sgx, f + 1)
                link(dve.tensor_scalar(t2[:, :], sgt[:, :], 1.0, None, ALU.add))
                dve.reciprocal(cf[:, :, NE], t2[:, :]).then_inc(s_coef, 1)

            def ffn(f):
                def low(u, h):
                    wait(dve, s_hh, UNITS * f + u + 1)
                    hh, hl = split_buffers(u, h)
                    to = hh[0:LAST, :] if is_last(u) else hl
                    dve.tensor_tensor(to, Hf[h][rows(u), :], hh[rows(u), :].bitcast(F32), ALU.subtract).then_inc(s_hl, 1)

                def turn(m):
                    for k in range(TURN):
                        if static(m, NM - 1):
                            ffn_turn(f, m, k, low, split_w1, split_w2)
                        if not static(m, 0) or k > 0:
                            hidden(f, m, k)
                        if not static(m, NM - 1):
                            ffn_turn(f, m, k, low, split_w1, split_w2)
                turns(dve, turn, NM - 1)
                ffn_tail(f, low, split_w2)
                for q in range(NQ):
                    h = q // 2
                    dve.wait_ge(s_l2, UNITS * (f + 1) - 1 + h)
                    dve.scalar_tensor_tensor(X[:, :, quarter(q)], ps[:, 2 * h:2 * h + 2, q % 2 * QUART:(q % 2 + 1) * QUART], 0.5,
                                             X[:, :, quarter(q)], ALU.mult, ALU.add).then_inc(s_xr, 1)

            def attention():
                norm(1)
                for i in range(4):
                    h, e = i // 2, i % 2
                    dve.wait_ge(a_sq, i + 1)
                    dve.tensor_tensor(Q[:, e, half(h)], ps[:, 4 + i, :], Q[:, e, half(h)], ALU.mult).then_inc(a_q, 1)
                for k in range(NH):
                    ins = dve.tensor_scalar(WO[:, k, :], WO[:, k, :], nw[:, k:k + 1], None, ALU.mult)
                ins.then_inc(a_wo, 1)
                dve.wait_ge(a_ones, 2)

                def sums(q):
                    dve.wait_ge(a_f, q + 1)
                    f = K[:, :, quarter(q)]
                    dve.tensor_scalar(f, f, -1.0, 1.0, ALU.mult, ALU.add)
                    for h in range(NH):
                        a = A[:, h, quarter(q)]
                        ins = dve.tensor_tensor_scan(a, ones, a, 0.0, ALU.mult, ALU.add)
                    ins.then_inc(a_A, 1)

                def values(b):
                    dve.wait_ge(a_vp, b + 1)
                    dve.tensor_copy(V[:, 2 * b:2 * b + 2, :], ps[:, b, :].rearrange("p (t n) -> p t n", n=D)).then_inc(a_v, 1)

                def decayed(t, p):
                    if static(t):
                        dve.wait_ge(a_e, t * P // QUART + 1)
                    wait(dve, a_sc, t - 1)
                    dve.tensor_tensor(Kg[p], K[:, :, bass.ts(t, P)], A[:, :, bass.ts(t, P)], ALU.mult).then_inc(a_kg, 1)
                    wait(dve, a_o, t - 1)
                    dve.tensor_tensor(Qd[p], Q[:, :, bass.ts(t, P)], E1[:, :, bass.ts(t, P)], ALU.mult).then_inc(a_qk, 1)

                def masked(t, p):
                    dve.copy_predicated(SM[p][:, :], tri2, ps[:, 2, 0:NH * P]).then_inc(a_sm, 1)

                def states(t, p):
                    wait(dve, a_st, t)
                    wait(dve, a_kv, t + 1)
                    for c in range(2):
                        dve.tensor_tensor(Su[:, :, :], ST[2 * p + c][:, :, :], kv_bank(c), ALU.add).then_inc(a_su, 1)
                        wait(dve, a_su, 2 * t + c + 1)
                        if c == 1 and not static(t, NT - 1):
                            wait(dve, a_sc, t + 2)
                        if c == 0:
                            wait(dve, a_dc, t + 1)
                        to = ST[(2 * p + c + 1) % 4]
                        for h in range(NH):
                            ins = dve.tensor_scalar(to[:, h, :], Su[:, h, :], DC[p][:, h, c:c + 1], None, ALU.mult)
                        ins.then_inc((a_s1, a_st)[c], 1)
                        if c == 0:
                            wait(dve, a_s1, t + 1)

                def step(t, p):
                    if not static(t, 0):
                        states(t - 1, 1 - p)
                    if static(t, 0):
                        dve.wait_ge(a_sc, 1)
                    if not static(t, NT):
                        masked(t, p)
                    if not static(t, NT) and not static(t, NT - 1):
                        decayed(t + 1, 1 - p)

                def turn(m):
                    for p in range(2):
                        step(2 * m + p, p)
                sums(0)
                for b in range(2):
                    values(b)
                sums(1)
                for b in range(2, 4):
                    values(b)
                dve.wait_ge(a_A, 2)
                dve.wait_ge(a_q, 4)
                decayed(0, 0)
                step(0, 0)
                sums(2)
                step(1, 1)
                sums(3)
                dve.wait_ge(a_A, NQ)
                dve.wait_ge(a_e, NQ)
                with dve.Fori(1, NT // 2 - 1) as m:
                    turn(m)
                turn(NT // 2 - 1)
                step(NT, 0)
                split_w1(1, 0, 0)
                for q in range(NQ):
                    dve.wait_ge(f_y, q + 1)
                    dve.wait_ge(f_r, q + 1)
                    y = ps[:, Y_BANK[q], :].rearrange("p (k n) -> p k n", k=KD)
                    dve.tensor_tensor(Yr[q], y, over_k(Or[q]), ALU.mult).then_inc(f_t, 1)
                    dve.wait_ge(f_t, q + 1)
                    dve.tensor_tensor(X[:, :, quarter(q)], X[:, :, quarter(q)], Yr[q], ALU.add).then_inc(s_xr, 1)
                    if q >= 2:
                        centre(2, q - 2)

            dve.memset(mean_of[:, :], 1.0 / D)
            dve.memset(zeros[:, :], 0.0)
            dve.memset(eps_ln[:, :], LN_EPS)
            dve.memset(eps_rms[:, :], RMS_EPS)
            dve.memset(one[:, :], 1.0).then_inc(s_set, 1)
            for a in range(2):
                dve.memset(cs[a][:, :, 0:NE], 0.0)
                dve.memset(SM[a][:, :], 0.0)
            link(dve.memset(ST[0][:, :, :], 0.0))
            norm(0)
            router(0)
            ffn(0)
            attention()
            norm(2, 2)
            router(1)
            ffn(1)


def layout(inputs):
    a = {k: np.asarray(v) for k, v in inputs.items()}

    def tiles(w):
        return np.ascontiguousarray(w.reshape(-1, P, w.shape[1]).transpose(1, 0, 2))

    w13, w2 = a["L0_ffn_w13"], a["L0_ffn_w2"]
    sgu, sd = a["L0_ffn_shared_gate_up_w"], a["L0_ffn_shared_down_w"]
    pad = np.zeros((NJ * P - NE * FE - FS, D), w13.dtype)
    gate = np.concatenate([w13[:, :FE].reshape(-1, D), sgu[:FS], pad])
    up = np.concatenate([w13[:, FE:].reshape(-1, D), sgu[FS:], pad])
    down = np.concatenate([w2.transpose(0, 2, 1).reshape(-1, D), sd.T, pad])
    w = np.empty((NJ, P, WC), w13.dtype)
    gate[-P + LAST:] = up[-P:-P + LAST]
    down[-P + LAST:] = down[-P:-P + LAST]
    for i, m in enumerate((gate, up)):
        part = m.reshape(NJ, P, KD, P).transpose(0, 3, 2, 1)
        w[:, :, i * KD * P:(i + 1) * KD * P] = part.reshape(NJ, P, KD * P)
    w[:, :, 2 * KD * P:] = down.reshape(NJ, P, D)

    s, t = np.arange(P)[:, None], np.arange(P)[None, :]
    same = s // CH == t // CH
    tri = (same & (s <= t)).astype(np.float32)
    c = np.zeros((P, C_ALL), np.float32)
    c[:, C_ID:C_ID + P] = np.eye(P)
    c[:, C_TRI:C_TRI + P] = tri
    c[:, C_TRI + P:C_TRI + 2 * P] = tri
    return {
        "xT": tiles(a["L0_attn_x"][0].T),
        "wffn": w,
        "wgate": tiles(np.concatenate([a["L0_ffn_gate_w"], a["L0_ffn_sgate_w"]]).T),
        "wkqv": tiles(np.concatenate([a["L0_attn_Wk"], a["L0_attn_Wq"], a["L0_attn_Wv"]]).T),
        "woT": tiles(a["L0_attn_Wo"].T),
        "normw": np.ascontiguousarray(a["L0_attn_norm_w"].reshape(NH, P).T),
        "consts": c,
    }


def kernel(**inputs):
    import concourse.bacc as bacc
    from concourse.bass_utils import run_bass_kernel_spmd

    nc = bacc.Bacc("TRN2", target_bir_lowering=False, num_devices=1)
    arrays = layout(inputs)
    args = [nc.dram_tensor(k, v.shape, mybir.dt.from_np(v.dtype), kind="ExternalInput").ap() for k, v in arrays.items()]
    out = nc.dram_tensor("out_t", (P, KD, N), F32, kind="ExternalOutput").ap()
    macaron(nc, *args, out)
    r = run_bass_kernel_spmd(nc, [arrays], core_ids=[0])
    y = r.results[0]["out_t"]
    return np.ascontiguousarray(y.transpose(2, 1, 0).reshape(1, N, D))
```
